# Optimizing a Trainium2 kernel written in Bass

```python
import numpy as np
import jax
import jax.numpy as jnp

def _softmax(x, axis=-1):
    return jax.nn.softmax(x, axis=axis)

def _gelu(x):
    return jax.nn.gelu(x, approximate=True)

def _silu(x):
    return jax.nn.silu(x)

def _sigmoid(x):
    return jax.nn.sigmoid(x)

def _layernorm(x, axis=-1, eps=1e-05):
    m = jnp.mean(x, axis=axis, keepdims=True)
    v = jnp.var(x, axis=axis, keepdims=True)
    return (x - m) / jnp.sqrt(v + eps)

def _scatter_add(tgt, idx, src, axis=0):
    return tgt.at[idx].add(src)

def _segment_sum(src, seg, n):
    return jax.ops.segment_sum(src, seg, n)
kernel_name = 'mk_xattn_seq_d1_seqx_r2_d8e81a'

def setup_inputs(seed: int=0):
    np.random.seed(seed)
    _w = jnp.asarray

    def _rec_inputs():
        import jax
        import jax.numpy as jnp
        _rk = jax.random.key(seed)
        x = -0.0002928 + 1 * jax.random.normal(jax.random.fold_in(_rk, 1), (32, 512, 512), jnp.float32)
        _lenS = 512 - jax.random.randint(jax.random.fold_in(_rk, 7), (32,), 0, max(1, 512 // 4) + 1, jnp.int32)
        _lenS2 = 77 - jax.random.randint(jax.random.fold_in(_rk, 8), (32,), 0, max(1, 77 // 4) + 1, jnp.int32)
        _ctx_1024P = jax.random.normal(jax.random.fold_in(_rk, 11), (32, 16, 512), jnp.float32)
        _ctx_1024c = jax.random.dirichlet(jax.random.fold_in(_rk, 511), 0.3 * jnp.ones((16,), jnp.float32), (32, 77))
        _ctx_1024t = jnp.einsum('bsk,bkd->bsd', _ctx_1024c, _ctx_1024P)
        _ctx_1024t = _ctx_1024t * jax.lax.rsqrt(jnp.mean(jnp.square(_ctx_1024t)) + 1e-12) * 0.953939
        ctx_1024 = -1.39393e-06 + 0.999914 * (_ctx_1024t + 0.3 * jax.random.normal(jax.random.fold_in(_rk, 611), (32, 77, 512), jnp.float32))
        _validS = jnp.arange(512)[None, :] < _lenS[:, None]
        _validS2 = jnp.arange(77)[None, :] < _lenS2[:, None]
        _causal = jnp.tril(jnp.ones((512, 512), dtype=bool))
        mask_BxS2_ik0 = jnp.where(jnp.broadcast_to(_validS2[:, :], (32, 77)), 0, 1).astype(jnp.int32)
        return (x, ctx_1024, mask_BxS2_ik0)
    x, ctx_1024, mask_BxS2_ik0 = _rec_inputs()

    def _L0_xattn_setup():
        import jax, jax.numpy as jnp
        import numpy as np
        PAD = float(-2 ** 32 + 1)
        NUM_HEADS = 16
        LN_EPS = 1e-05

        def _split_heads(x, h):
            B, T, D = x.shape
            d = D // h
            return x.reshape(B, T, h, d).transpose(2, 0, 1, 3).reshape(h * B, T, d)

        def _merge_heads(x, h):
            hB, T, d = x.shape
            B = hB // h
            return x.reshape(h, B, T, d).transpose(1, 2, 0, 3).reshape(B, T, h * d)
        key = jax.random.key(seed)
        ks = jax.random.split(key, 12)
        B, T, D = (2, 1024, 512)
        s = 1.0 / np.sqrt(D)
        return {'q': jax.random.normal(ks[0], (B, T, D), jnp.float32), 'k': jax.random.normal(ks[1], (B, T, D), jnp.float32), 'v': jax.random.normal(ks[2], (B, T, D), jnp.float32), 'mask': jax.random.randint(ks[3], (B, T), 0, 2, jnp.int32), 'causality': 0, 'edge_fea': jnp.zeros((1,), jnp.float32), 'wq': jax.random.normal(ks[4], (D, D), jnp.float32) * s, 'bq': jax.random.normal(ks[5], (D,), jnp.float32) * 0.01, 'wk': jax.random.normal(ks[6], (D, D), jnp.float32) * s, 'bk': jax.random.normal(ks[7], (D,), jnp.float32) * 0.01, 'wv': jax.random.normal(ks[8], (D, D), jnp.float32) * s, 'bv': jax.random.normal(ks[9], (D,), jnp.float32) * 0.01, 'gamma': jnp.ones((D,), jnp.float32), 'beta': jnp.zeros((D,), jnp.float32)}
    _L0_xattn_all = _L0_xattn_setup()
    _L0_xattn_in = {k: v for k, v in _L0_xattn_all.items() if k in ('edge_fea', 'wq', 'bq', 'wk', 'bk', 'wv', 'bv', 'gamma', 'beta')}
    del _L0_xattn_all
    return {'x': x, 'ctx_1024': ctx_1024, 'mask_BxS2_ik0': mask_BxS2_ik0, 'L0_xattn_edge_fea': _L0_xattn_in['edge_fea'], 'L0_xattn_wq': _L0_xattn_in['wq'], 'L0_xattn_bq': _L0_xattn_in['bq'], 'L0_xattn_wk': _L0_xattn_in['wk'], 'L0_xattn_bk': _L0_xattn_in['bk'], 'L0_xattn_wv': _L0_xattn_in['wv'], 'L0_xattn_bv': _L0_xattn_in['bv'], 'L0_xattn_gamma': _L0_xattn_in['gamma'], 'L0_xattn_beta': _L0_xattn_in['beta']}

def reference(x, ctx_1024, mask_BxS2_ik0, L0_xattn_edge_fea, L0_xattn_wq, L0_xattn_bq, L0_xattn_wk, L0_xattn_bk, L0_xattn_wv, L0_xattn_bv, L0_xattn_gamma, L0_xattn_beta):
    import jax
    import jax.numpy as jnp

    def _L0_xattn_ref(q, k, v, mask, causality, edge_fea, wq, bq, wk, bk, wv, bv, gamma, beta):
        import jax, jax.numpy as jnp
        import numpy as np
        PAD = float(-2 ** 32 + 1)
        NUM_HEADS = 16
        LN_EPS = 1e-05

        def _split_heads(x, h):
            B, T, D = x.shape
            d = D // h
            return x.reshape(B, T, h, d).transpose(2, 0, 1, 3).reshape(h * B, T, d)

        def _merge_heads(x, h):
            hB, T, d = x.shape
            B = hB // h
            return x.reshape(h, B, T, d).transpose(1, 2, 0, 3).reshape(B, T, h * d)
        h = NUM_HEADS
        B, T, D = q.shape
        depth = D // h
        qh = _split_heads(q @ wq.T + bq, h)
        kh = _split_heads(k @ wk.T + bk, h)
        vh = _split_heads(v @ wv.T + bv, h)
        scores = jnp.einsum('ntd,nsd->nts', qh, kh) / jnp.sqrt(jnp.asarray(depth, qh.dtype))
        km = jnp.repeat(mask.astype(scores.dtype), h, axis=0)[:, None, :]
        scores = scores + km * PAD
        if causality:
            tril = jnp.tril(jnp.ones((T, T), scores.dtype))
            scores = jnp.where(tril[None] == 0, jnp.full_like(scores, PAD), scores)
        attn = jax.nn.softmax(scores, axis=-1)
        ctx = jnp.einsum('nts,nsd->ntd', attn, vh)
        out = _merge_heads(ctx, h) + q
        mu = jnp.mean(out, axis=-1, keepdims=True)
        var = jnp.var(out, axis=-1, keepdims=True)
        out = (out - mu) / jnp.sqrt(var + LN_EPS) * gamma + beta
        return out
    x = _L0_xattn_ref(x, ctx_1024, ctx_1024, mask_BxS2_ik0, 0, L0_xattn_edge_fea, L0_xattn_wq, L0_xattn_bq, L0_xattn_wk, L0_xattn_bk, L0_xattn_wv, L0_xattn_bv, L0_xattn_gamma, L0_xattn_beta)
    return x

_drawn_inputs = setup_inputs


def setup_inputs(seed=0):
    import zlib

    import numpy as np

    out = dict(_drawn_inputs(seed))
    spreads = {'L0_xattn_gamma': (1.0, 0.2), 'L0_xattn_beta': (0.0, 0.1)}
    factors = {'L0_xattn_bq': 26.915, 'L0_xattn_bk': 64.0, 'L0_xattn_bv': 6.653}
    for name, (base, spread) in spreads.items():
        noise = np.random.default_rng([zlib.crc32(name.encode()), seed]).standard_normal(out[name].shape)
        drawn = base * np.exp(spread * noise) if base else spread * noise
        out[name] = jnp.asarray(drawn.astype(out[name].dtype))
    for name, factor in factors.items():
        out[name] = (out[name] * factor).astype(out[name].dtype)
    return out
```

```python
from contextlib import ExitStack

import concourse.bass as bass
from concourse import mybir

F32 = mybir.dt.float32
F32R = mybir.dt.float32r
I32 = mybir.dt.int32
ALU = mybir.AluOpType
ACT = mybir.ActivationFunctionType
AX = mybir.AxisListType

P = 128
HEADS = 16
PAD = float(-2**32 + 1)
LN_EPS = 1e-5
BANK = 512
DMA = 16


def at_least(eng, sem, value):
    if isinstance(value, int) and value <= 0:
        return
    eng.wait_ge(sem, value)


def xattn(nc, x, xT, ctxT, mask, wqT, bq, wkT, bk, wvT, bv, gamma, beta, out):
    B, T, D = x.shape
    S = mask.shape[1] // HEADS
    DH = D // HEADS
    KC = D // P
    NG = D // P
    HG = HEADS // NG
    TT = T // P
    HH = HEADS // 2
    ROWS = HH * S
    NT = -(-ROWS // P)
    VW = DH + 1
    SCALE = float(DH) ** -0.5
    GS = HG * S
    CB = 4
    CR = CB * S
    VROWS = [103, 103, 102]
    assert sum(VROWS) == CR and D == 512 and T == 512 and B % CB == 0

    tile_rows = [min(P, ROWS - P * i) for i in range(NT)]
    first_head = [P * i // S for i in range(NT)]
    last_head = [(P * i + tile_rows[i] - 1) // S for i in range(NT)]
    tile_cols = [(last_head[i] - first_head[i] + 1) * VW for i in range(NT)]
    VCOLS = max(tile_cols)
    pieces = []
    for i in range(NT):
        for hd in range(first_head[i], last_head[i] + 1):
            lo, hi = max(P * i, hd * S), min(P * i + tile_rows[i], (hd + 1) * S)
            pieces.append((i, lo - P * i, hd, lo - hd * S, hi - lo))

    k_dram = nc.dram_tensor("k_scratch", (B, P, NG, S), F32, kind="Internal").ap()
    v_dram = nc.dram_tensor("v_scratch", (B * S, HEADS * VW), F32, kind="Internal").ap()
    v_rows = v_dram.rearrange("(b s) (h w) -> b s h w", s=S, w=VW)

    with ExitStack() as whole:
        def sb(where, name, shape, dt):
            return where.enter_context(nc.sbuf_tensor(name, shape, dt))

        def ps(where, name, shape):
            return where.enter_context(nc.psum_tensor(name, shape, F32))

        def sem(name):
            return whole.enter_context(nc.semaphore(name))

        wq_hi = sb(whole, "wq_hi", [P, KC, D], F32R)
        wq_lo = sb(whole, "wq_lo", [P, KC, D], F32R)
        bq_col = sb(whole, "bq_col", [P, NG], F32)
        gamma_all = sb(whole, "gamma_all", [P, D], F32)
        beta_all = sb(whole, "beta_all", [P, D], F32)
        ident = sb(whole, "ident", [P, P], F32)
        mask_pad = [sb(whole, f"mask_pad{i}", [P, HEADS * S], F32) for i in range(2)]

        w_loaded = [sem(f"w_loaded_{n}") for n in "kvq"]
        consts_loaded = sem("consts_loaded")
        w_hi_ready = [sem(f"w_hi_ready_{n}") for n in "kvq"]
        w_lo_ready = [sem(f"w_lo_ready_{n}") for n in "kvq"]
        bk_scaled = sem("bk_scaled")
        ones_set = sem("ones_set")
        ident_zero = sem("ident_zero")
        ident_set = sem("ident_set")
        ctx_loaded = [sem(f"ctx_loaded_{i}") for i in range(2)]
        mask_loaded = sem("mask_loaded")
        mask_ready = sem("mask_ready")
        ctx_hi_ready = sem("ctx_hi_ready")
        ctx_lo_ready = sem("ctx_lo_ready")
        k_done = sem("k_done")
        v_done = sem("v_done")
        k_copied = sem("k_copied")
        v_copied = sem("v_copied")
        k_stored = [sem(f"k_stored_{i}") for i in range(2)]
        v_stored = [sem(f"v_stored_{i}") for i in range(2)]
        CHUNKS = B // CB

        with ExitStack() as one:
            w_raw = [sb(one, f"w_raw_{n}", [P, KC, D], F32) for n in "kvq"]
            wk_hi = sb(one, "wk_hi", [P, KC, D], F32R)
            wk_lo = sb(one, "wk_lo", [P, KC, D], F32R)
            wv_hi = sb(one, "wv_hi", [P, KC, D], F32R)
            wv_lo = sb(one, "wv_lo", [P, KC, D], F32R)
            mask_raw = sb(one, "mask_raw", [P, 2, HEADS * S], I32)
            bk_col = sb(one, "bk_col", [P, NG], F32)
            bk_sc = sb(one, "bk_sc", [P, NG], F32)
            bv_all = sb(one, "bv_all", [P, D], F32)
            ctx_raw = [sb(one, f"ctx_raw{i}", [P, KC, CR], F32) for i in range(2)]
            ctx_hi = [sb(one, f"ctx_hi{i}", [P, KC, CR], F32R) for i in range(2)]
            ctx_lo = [sb(one, f"ctx_lo{i}", [P, KC, CR], F32R) for i in range(2)]
            k_out = [sb(one, f"k_out{i}", [P, NG, CR], F32) for i in range(2)]
            v_out = [sb(one, f"v_out{i}", [P, 3, HEADS, VW], F32) for i in range(2)]
            k_ps = [ps(one, f"k_ps{i}", [P, BANK]) for i in range(NG)]
            v_ps = [ps(one, f"v_ps{i}", [P, BANK]) for i in range(3)]
            his = [wk_hi, wv_hi, wq_hi]
            los = [wk_lo, wv_lo, wq_lo]

            def of_parity(c, par, each):
                return c * (each // 2) - par * (each // 2)

            def chunk_loop(eng, body):
                body(0, 0)
                body(1, 1)
                with eng.Fori(1, CHUNKS // 2) as pair:
                    body(pair * 2, 0)
                    body(pair * 2 + 1, 1)

            block = one.enter_context(nc.Block())

            @block.sync
            def _(sp):
                ctx_src = ctxT.rearrange("(k p) c r -> p k c r", p=P)
                sp.dma_start(w_raw[0][:], wkT.rearrange("(k p) n -> p k n", p=P)).then_inc(w_loaded[0], DMA)
                sp.dma_start(bk_col[:], bk).then_inc(consts_loaded, DMA)
                sp.dma_start(bq_col[:], bq).then_inc(consts_loaded, DMA)

                def load(c, par):
                    at_least(sp, ctx_hi_ready, c - 1)
                    at_least(sp, ctx_lo_ready, c - 1)
                    sp.dma_start(ctx_raw[par][:], ctx_src[:, :, c, :]).then_inc(ctx_loaded[par], DMA)

                load(0, 0)
                sp.dma_start(w_raw[1][:], wvT.rearrange("(k p) n -> p k n", p=P)).then_inc(w_loaded[1], DMA)
                load(1, 1)
                sp.dma_start(bv_all[:], bv.partition_broadcast(P)).then_inc(consts_loaded, DMA)
                sp.dma_start(w_raw[2][:], wqT.rearrange("(k p) n -> p k n", p=P)).then_inc(w_loaded[2], DMA)
                sp.dma_start(gamma_all[:], gamma.partition_broadcast(P)).then_inc(consts_loaded, DMA)
                sp.dma_start(beta_all[:], beta.partition_broadcast(P)).then_inc(consts_loaded, DMA)
                sp.dma_start(mask_raw[:], mask.partition_broadcast(P)).then_inc(mask_loaded, DMA)

                def store(c, par):
                    for m in range(NG):
                        sp.wait_ge(k_copied, c * NG + (m + 1))
                        sp.dma_start(k_dram[bass.ds(c * CB, CB), :, m, :].rearrange("b p s -> p b s"),
                                     k_out[par][:, m, :].rearrange("p (b s) -> p b s", b=CB)
                                     ).then_inc(k_stored[par], DMA)
                    for j in range(3):
                        sp.wait_ge(v_copied, c * 3 + (j + 1))
                        sp.dma_start(v_dram[bass.ds(c * CR + 103 * j, VROWS[j]), :],
                                     v_out[par][0:VROWS[j], j, :, :].rearrange("p h w -> p (h w)")
                                     ).then_inc(v_stored[par], DMA)

                load(2, 0)
                store(0, 0)
                load(3, 1)
                store(1, 1)
                with sp.Fori(1, CHUNKS // 2 - 1) as pair:
                    load(pair * 2 + 2, 0)
                    store(pair * 2, 0)
                    load(pair * 2 + 3, 1)
                    store(pair * 2 + 1, 1)
                store(CHUNKS - 2, 0)
                store(CHUNKS - 1, 1)
                for par in range(2):
                    sp.wait_ge(k_stored[par], DMA * NG * CHUNKS // 2)
                    sp.wait_ge(v_stored[par], DMA * 3 * CHUNKS // 2)

            @block.gpsimd
            def _(pool):
                pool.memset(ident[:], 0.0).then_inc(ident_zero, 1)
                pool.wait_ge(ident_zero, 1)
                pool.affine_select(out=ident[:], in_=ident[:], compare_op=ALU.not_equal, fill=1.0,
                                   base=0, pattern=[[-1, P]], channel_multiplier=1).then_inc(ident_set, 1)
                for par in range(2):
                    pool.memset(v_out[par][:, :, :, DH:VW], 1.0).then_inc(ones_set, 1)
                pool.wait_ge(w_loaded[2], DMA)
                pool.wait_ge(w_hi_ready[2], 1)
                pool.tensor_tensor(wq_lo[:], w_raw[2][:], wq_hi[:], ALU.subtract).then_inc(w_lo_ready[2], 1)
                pool.wait_ge(mask_loaded, DMA)
                for i in range(2):
                    pool.tensor_scalar(mask_pad[i][:], mask_raw[:, i, :], PAD, None, ALU.mult
                                       ).then_inc(mask_ready, 1)
                pool.wait_ge(ident_set, 1)
                pool.wait_ge(w_lo_ready[2], 1)
                pool.wait_ge(mask_ready, 2)

            @block.scalar
            def _(act):
                def chunk(c, par):
                    act.wait_ge(ctx_loaded[par], of_parity(c, par, DMA) + DMA)
                    at_least(act, k_done, c * NG - NG)
                    at_least(act, v_done, c * 3 - 3)
                    act.copy(ctx_hi[par][:], ctx_raw[par][:]).then_inc(ctx_hi_ready, 1)

                def keys(c, par):
                    at_least(act, k_stored[par], of_parity(c, par, DMA * NG))
                    for m in range(NG):
                        act.wait_ge(k_done, c * NG + (m + 1))
                        act.activation(k_out[par][:, m, :], k_ps[m][:, 0:CR], ACT.Identity,
                                       bias=bk_sc[:, m:m + 1], scale=SCALE).then_inc(k_copied, 1)

                chunk(0, 0)
                act.wait_ge(w_loaded[2], DMA)
                act.copy(wq_hi[:], w_raw[2][:]).then_inc(w_hi_ready[2], 1)
                chunk(1, 1)
                act.wait_ge(bk_scaled, 1)
                keys(0, 0)
                with act.Fori(0, CHUNKS // 2 - 1) as pair:
                    chunk(pair * 2 + 2, 0)
                    keys(pair * 2 + 1, 1)
                    chunk(pair * 2 + 3, 1)
                    keys(pair * 2 + 2, 0)
                keys(CHUNKS - 1, 1)

            @block.vector
            def _(dve):
                for n in range(2):
                    if n == 1:
                        dve.wait_ge(consts_loaded, 5 * DMA)
                        dve.tensor_scalar(bk_sc[:], bk_col[:], SCALE, None, ALU.mult).then_inc(bk_scaled, 1)
                    dve.wait_ge(w_loaded[n], DMA)
                    dve.tensor_copy(his[n][:], w_raw[n][:]).then_inc(w_hi_ready[n], 1)
                    dve.wait_ge(w_hi_ready[n], 1)
                    dve.tensor_tensor(los[n][:], w_raw[n][:], his[n][:], ALU.subtract).then_inc(w_lo_ready[n], 1)
                    if n == 0:
                        dve.wait_ge(ctx_hi_ready, 1)
                        dve.tensor_tensor(ctx_lo[0][:], ctx_raw[0][:], ctx_hi[0][:], ALU.subtract
                                          ).then_inc(ctx_lo_ready, 1)

                def low(c, par):
                    dve.wait_ge(ctx_hi_ready, c + 1)
                    dve.tensor_tensor(ctx_lo[par][:], ctx_raw[par][:], ctx_hi[par][:], ALU.subtract
                                      ).then_inc(ctx_lo_ready, 1)

                def values(c, par):
                    at_least(dve, v_stored[par], of_parity(c, par, DMA * 3))
                    for j in range(3):
                        n = VROWS[j]
                        dve.wait_ge(v_done, c * 3 + (j + 1))
                        dve.tensor_tensor(v_out[par][0:n, j, :, 0:DH],
                                          v_ps[j][0:n, :].rearrange("p (h w) -> p h w", h=HEADS),
                                          bv_all[0:n, :].rearrange("p (h w) -> p h w", h=HEADS),
                                          ALU.add).then_inc(v_copied, 1)

                low(1, 1)
                dve.wait_ge(ones_set, 2)
                values(0, 0)
                with dve.Fori(0, CHUNKS // 2 - 1) as pair:
                    low(pair * 2 + 2, 0)
                    values(pair * 2 + 1, 1)
                    low(pair * 2 + 3, 1)
                    values(pair * 2 + 2, 0)
                values(CHUNKS - 1, 1)

            @block.tensor
            def _(pe):
                def project(c, par):
                    if isinstance(c, int) and c == 0:
                        pe.wait_ge(w_hi_ready[0], 1)
                        pe.wait_ge(w_lo_ready[0], 1)
                    pe.wait_ge(ctx_hi_ready, c + 1)
                    pe.wait_ge(ctx_lo_ready, c + 1)
                    terms = [(0, 1), (1, 0), (0, 0)]
                    c_part = (ctx_hi[par], ctx_lo[par])
                    for m in range(NG):
                        at_least(pe, k_copied, c * NG + (m + 1 - NG))
                        for k in range(KC):
                            for n, (a, b) in enumerate(terms):
                                mm = pe.matmul(k_ps[m][:, 0:CR], (wk_hi, wk_lo)[a][:, k, P * m:P * m + P],
                                               c_part[b][:, k, :], start=(k == 0 and n == 0),
                                               stop=(k == KC - 1 and n == 2))
                        mm.then_inc(k_done, 1)
                    if isinstance(c, int) and c == 0:
                        pe.wait_ge(w_hi_ready[1], 1)
                        pe.wait_ge(w_lo_ready[1], 1)
                    for j in range(3):
                        at_least(pe, v_copied, c * 3 + (j + 1 - 3))
                        for k in range(KC):
                            for n, (a, b) in enumerate(terms):
                                mm = pe.matmul(v_ps[j][0:VROWS[j], :],
                                               c_part[a][:, k, 103 * j:103 * j + VROWS[j]],
                                               (wv_hi, wv_lo)[b][:, k, :], start=(k == 0 and n == 0),
                                               stop=(k == KC - 1 and n == 2))
                        mm.then_inc(v_done, 1)

                chunk_loop(pe, project)

        xT_loaded = sem("xT_loaded")
        k_loaded = sem("k_loaded")
        v_loaded = [sem(f"v_loaded_{h}") for h in range(2)]
        x_loaded = sem("x_loaded")
        out_stored = [sem(f"out_stored_{i}") for i in range(2)]
        x_hi_ready = sem("x_hi_ready")
        x_lo_ready = sem("x_lo_ready")
        q_done = sem("q_done")
        q_hi_ready = sem("q_hi_ready")
        q_lo_ready = sem("q_lo_ready")
        zeros_set = sem("zeros_set")
        bd_hi_ready = sem("bd_hi_ready")
        bd_lo_ready = sem("bd_lo_ready")
        scores_done = sem("scores_done")
        masked = sem("masked")
        max_ready = sem("max_ready")
        shifted = sem("shifted")
        exp_done = sem("exp_done")
        turned = sem("turned")
        pt_ready = sem("pt_ready")
        pv_done = sem("pv_done")
        inv_ready = sem("inv_ready")
        attn_ready = sem("attn_ready")
        resid_done = sem("resid_done")
        stats_done = sem("stats_done")
        meanvar_done = sem("meanvar_done")
        var_ready = sem("var_ready")
        half_set = sem("half_set")
        rstd_ready = sem("rstd_ready")
        shift_ready = sem("shift_ready")
        normed = sem("normed")
        scaled = sem("scaled")
        out_ready = sem("out_ready")

        with ExitStack() as two:
            xT_raw = sb(two, "xT_raw", [P, KC, T], F32)
            x_hi = [sb(two, f"x_hi{i}", [P, KC, T], F32R) for i in range(2)]
            x_lo = [sb(two, f"x_lo{i}", [P, KC, T], F32R) for i in range(2)]
            q_hi = sb(two, "q_hi", [P, NG, T], F32R)
            q_lo = sb(two, "q_lo", [P, NG, T], F32R)
            k_raw = sb(two, "k_raw", [P, NG, S], F32)
            bd_hi = [sb(two, f"bd_hi{i}", [P, NG, HG, S], F32R) for i in range(2)]
            bd_lo = [sb(two, f"bd_lo{i}", [P, NG, HG, S], F32R) for i in range(2)]
            probs = [sb(two, f"probs{h}", [P, TT, ROWS], F32) for h in range(2)]
            row_max = sb(two, "row_max", [P, 2 * TT, HH], F32)
            pt = [sb(two, f"pt{h}", [P, NT, T], F32) for h in range(2)]
            v_tiles = [sb(two, f"v_tiles{h}", [P, NT, VCOLS], F32) for h in range(2)]
            inv_sum = sb(two, "inv_sum", [P, 2 * TT, HH], F32)
            x_rows = sb(two, "x_rows", [P, TT, D], F32)
            attn = [sb(two, f"attn{i}", [P, TT, D], F32) for i in range(2)]
            y = [sb(two, f"y{i}", [P, TT, D], F32) for i in range(2)]
            stats = sb(two, "stats", [P, TT, 6], F32)
            meanvar = sb(two, "meanvar", [P, TT, 2], F32)
            var_eps = sb(two, "var_eps", [P, TT], F32)
            neg_mean = sb(two, "neg_mean", [P, TT], F32)
            minus_half = sb(two, "minus_half", [P, TT], F32)
            rstd = sb(two, "rstd", [P, TT], F32)
            shift = sb(two, "shift", [P, TT], F32)
            s_ps = [ps(two, f"s_ps{i}", [P, 2, BANK]) for i in range(2)]
            t_ps = [ps(two, f"t_ps{i}", [P, BANK]) for i in range(2)]
            q_ps = ps(two, "q_ps", [P, BANK])
            o_ps = ps(two, "o_ps", [P, BANK])

            def real(b):
                return not isinstance(b, int) or 0 <= b < B

            def steps(eng, body, first=-1):
                for a in range(first, 4):
                    body(a, a % 2)
                with eng.Fori(2, B // 2 - 1) as pair:
                    body(pair * 2, 0)
                    body(pair * 2 + 1, 1)
                for a in range(B - 2, B + 3):
                    body(a, a % 2)

            block = two.enter_context(nc.Block())

            @block.sync
            def _(sp):
                def load_v(b, h):
                    at_least(sp, pv_done, b * 8 + (4 * h - 4))
                    if isinstance(b, int) and b == 0:
                        sp.wait_ge(zeros_set, 6)
                    for i, row, hd, key, n in pieces:
                        col = (hd - first_head[i]) * VW
                        sp.dma_start(v_tiles[h][row:row + n, i, col:col + VW],
                                     v_rows[b, key:key + n, HH * h + hd, :]).then_inc(v_loaded[h], DMA)

                def store(b, t, par):
                    sp.wait_ge(out_ready, b * 4 + (t + 1))
                    sp.dma_start(out[b, P * t:P * t + P, :], y[par][:, t, :]).then_inc(out_stored[par], DMA)

                def step(a, par):
                    if real(a + 2):
                        at_least(sp, x_hi_ready, a * 4 + 8)
                        at_least(sp, x_lo_ready, a * 4 + 8)
                        sp.dma_start(xT_raw[:], xT[a + 2].rearrange("(k p) t -> p k t", p=P)
                                     ).then_inc(xT_loaded, DMA)
                    if real(a - 1):
                        load_v(a - 1, 1)
                        at_least(sp, resid_done, a * 4 - 4)
                        sp.dma_start(x_rows[:], x[a - 1].rearrange("(t p) d -> p t d", p=P)
                                     ).then_inc(x_loaded, DMA)
                    if real(a - 3):
                        store(a - 3, 2, 1 - par)
                        store(a - 3, 3, 1 - par)
                    if real(a):
                        load_v(a, 0)
                    if real(a - 2):
                        store(a - 2, 0, par)
                    if real(a + 2):
                        at_least(sp, bd_hi_ready, a * 4 + 8)
                        at_least(sp, bd_lo_ready, a * 4 + 8)
                        sp.dma_start(k_raw[:], k_dram[a + 2]).then_inc(k_loaded, DMA)
                    if real(a - 2):
                        store(a - 2, 1, par)

                steps(sp, step, first=-2)
                for par in range(2):
                    sp.wait_ge(out_stored[par], DMA * TT * B // 2)

            @block.tensor
            def _(pe):
                terms = [(0, 1), (1, 0), (0, 0)]

                def q_half(b, g, part, par):
                    if part == 0:
                        pe.wait_ge(x_hi_ready, b * 4 + 4)
                        pe.wait_ge(x_lo_ready, b * 4 + 4)
                        at_least(pe, q_hi_ready, b * 4 + g)
                        at_least(pe, q_lo_ready, b * 4 + g)
                    x_part = (x_hi[par], x_lo[par])
                    for k in (2 * part, 2 * part + 1):
                        for n, (u, v) in enumerate(terms):
                            mm = pe.matmul(q_ps[:, :], (wq_hi, wq_lo)[u][:, k, P * g:P * g + P],
                                           x_part[v][:, k, :], start=(k == 0 and n == 0),
                                           stop=(k == KC - 1 and n == 2))
                    if part == 1:
                        mm.then_inc(q_done, 1)

                def scores(b, h, t, par):
                    pe.wait_ge(q_hi_ready, b * 4 + (2 * h + 2))
                    pe.wait_ge(q_lo_ready, b * 4 + (2 * h + 2))
                    pe.wait_ge(bd_hi_ready, b * 4 + 4)
                    pe.wait_ge(bd_lo_ready, b * 4 + 4)
                    at_least(pe, masked, b * 8 + (4 * h + t - 1))
                    for j in range(2):
                        g = 2 * h + j
                        for n, (u, v) in enumerate(terms):
                            mm = pe.matmul(s_ps[t % 2][:, j, 0:GS], (q_hi, q_lo)[u][:, g, P * t:P * t + P],
                                           (bd_hi, bd_lo)[v][par][:, g, :, :].rearrange("p h s -> p (h s)"),
                                           start=(n == 0), stop=(n == 2))
                    mm.then_inc(scores_done, 1)

                def turn(b, h, i):
                    pe.wait_ge(exp_done, b * 8 + (4 * h + 4))
                    at_least(pe, pt_ready, b * (2 * NT) + (NT * h + i - 1))
                    w = tile_rows[i]
                    for t in range(TT):
                        mm = pe.transpose(t_ps[(NT * h + i) % 2][0:w, P * t:P * t + P],
                                          probs[h][:, t, P * i:P * i + w], ident[:, :])
                    mm.then_inc(turned, 1)

                def product(b, h, t):
                    pe.wait_ge(pt_ready, b * (2 * NT) + (NT * h + NT))
                    pe.wait_ge(v_loaded[h], (b + 1) * (DMA * len(pieces)))
                    at_least(pe, attn_ready, b * 8 + (4 * h + t))
                    for i in range(NT):
                        w, col = tile_rows[i], first_head[i] * VW
                        mm = pe.matmul(o_ps[:, col:col + tile_cols[i]], pt[h][0:w, i, P * t:P * t + P],
                                       v_tiles[h][0:w, i, 0:tile_cols[i]], start=(i == 0),
                                       stop=(i == NT - 1), skip_group_check=True)
                    mm.then_inc(pv_done, 1)

                def step(a, par):
                    for s in range(8):
                        h, t = s // 4, s % 4
                        qb = a + h
                        if real(qb):
                            q_half(qb, (2 if h == 0 else 0) + t // 2, t % 2, (par + h) % 2)
                        if real(a):
                            scores(a, h, t, par)
                        if real(a - 1 + h):
                            for i in ([], [0, 1], [2, 3], [4])[t]:
                                turn(a - 1 + h, 1 - h, i)
                        if real(a - 1):
                            product(a - 1, h, t)

                steps(pe, step)

            @block.vector
            def _(dve):
                o_heads = o_ps[:, 0:HH * VW].rearrange("p (h w) -> p h w", w=VW)
                dve.memset(bd_hi[0][:].bitcast(F32), 0.0).then_inc(zeros_set, 1)
                dve.memset(bd_hi[1][:].bitcast(F32), 0.0).then_inc(zeros_set, 1)
                dve.memset(bd_lo[0][:].bitcast(F32), 0.0).then_inc(zeros_set, 1)
                dve.memset(bd_lo[1][:].bitcast(F32), 0.0).then_inc(zeros_set, 1)
                dve.memset(v_tiles[0][:], 0.0).then_inc(zeros_set, 1)
                dve.memset(v_tiles[1][:], 0.0).then_inc(zeros_set, 1)
                dve.wait_ge(zeros_set, 6)

                def invert_sums(b, h, t):
                    u = 4 * h + t
                    dve.wait_ge(pv_done, b * 8 + (u + 1))
                    dve.reciprocal(inv_sum[:, u, :], o_heads[:, :, DH]).then_inc(inv_ready, 1)

                def scale_attn(b, h, t, par):
                    u = 4 * h + t
                    dve.wait_ge(inv_ready, b * 8 + (u + 1))
                    if h == 0:
                        at_least(dve, scaled, b * 4 + (t - 7))
                    dve.tensor_tensor(attn[par][:, t, HH * DH * h:HH * DH * (h + 1)].rearrange(
                                          "p (h w) -> p h w", w=DH),
                                      o_heads[:, :, 0:DH],
                                      inv_sum[:, u, :].unsqueeze(2).broadcast_to([P, HH, DH]),
                                      ALU.mult).then_inc(attn_ready, 1)

                def row_stats(b, t, par):
                    dve.wait_ge(resid_done, b * 4 + (t + 1))
                    dve.bn_stats(stats[:, t, :], attn[par][:, t, :]).then_inc(stats_done, 1)

                def mean_and_var(b, t):
                    dve.bn_aggr(meanvar[:, t, :], stats[:, t, :]).then_inc(meanvar_done, 1)

                def row_factors(b):
                    dve.wait_ge(meanvar_done, b * 4 + 4)
                    at_least(dve, normed, b * 4)
                    dve.tensor_scalar(var_eps[:], meanvar[:, :, 1], LN_EPS, None, ALU.add
                                      ).then_inc(var_ready, 1)
                    dve.tensor_scalar(neg_mean[:], meanvar[:, :, 0], -1.0, None, ALU.mult
                                      ).then_inc(var_ready, 1)

                def split_x(b, k, par):
                    dve.wait_ge(x_hi_ready, b * 4 + (k + 1))
                    dve.tensor_tensor(x_lo[par][:, k, :], xT_raw[:, k, :], x_hi[par][:, k, :], ALU.subtract
                                      ).then_inc(x_lo_ready, 1)

                def low_keys(b, q, par):
                    rows = slice(DH * q, DH * q + DH)
                    dve.wait_ge(bd_hi_ready, b * 4 + (q + 1))
                    dve.tensor_tensor(bd_lo[par][rows, :, q, :], k_raw[rows, :, :], bd_hi[par][rows, :, q, :],
                                      ALU.subtract).then_inc(bd_lo_ready, 1)

                def q_low(b, g):
                    dve.wait_ge(q_hi_ready, b * 4 + (g + 1))
                    dve.scalar_tensor_tensor(out=q_lo[:, g, :], in0=q_ps[:, :], scalar=bq_col[:, g:g + 1],
                                             in1=q_hi[:, g, :], op0=ALU.add, op1=ALU.subtract
                                             ).then_inc(q_lo_ready, 1)

                def add_mask(b, h, t, par):
                    u = 4 * h + t
                    dve.wait_ge(scores_done, b * 8 + (u + 1))
                    if t == 0:
                        at_least(dve, turned, b * (2 * NT) + (NT * h - NT))
                    dve.tensor_tensor(probs[h][:, t, :].rearrange("p (j c) -> p j c", j=2),
                                      s_ps[t % 2][:, :, 0:GS],
                                      mask_pad[par][:, ROWS * h:ROWS * h + ROWS].rearrange("p (j c) -> p j c", j=2),
                                      ALU.add).then_inc(masked, 1)

                def maximum(b, h, t):
                    u = 4 * h + t
                    dve.wait_ge(masked, b * 8 + (u + 1))
                    dve.tensor_reduce(row_max[:, u, :], probs[h][:, t, :].rearrange("p (h s) -> p h s", h=HH),
                                      AX.X, ALU.max).then_inc(max_ready, 1)

                def step(a, par):
                    for s in range(8):
                        h, t = s // 4, s % 4
                        last = None
                        if s == 0 and real(a - 2):
                            last = (a - 2, 1, 3)
                        if s > 0 and real(a - 1):
                            last = (a - 1, (s - 1) // 4, (s - 1) % 4)
                        if last is not None:
                            invert_sums(*last)
                        if 1 <= s <= 4 and real(a + 1):
                            low_keys(a + 1, s - 1, 1 - par)
                        if last is not None:
                            scale_attn(*last, par if s == 0 else 1 - par)
                        if real(a + h) and t % 2 == 1:
                            q_low(a + h, (2 if h == 0 else 0) + t // 2)
                        if real(a):
                            add_mask(a, h, t, par)
                        if h == 1 and real(a + 2):
                            split_x(a + 2, t, par)
                        rows = None
                        if real(a - 2) and s < 2:
                            rows = (a - 2, 2 + s)
                            row_stats(*rows, par)
                        if real(a - 1) and s >= 6:
                            rows = (a - 1, s - 6)
                            row_stats(*rows, 1 - par)
                        if rows is not None:
                            dve.wait_ge(stats_done, rows[0] * 4 + (rows[1] + 1))
                        if real(a):
                            maximum(a, h, t)
                        if rows is not None:
                            mean_and_var(*rows)
                        if s == 1 and real(a - 2):
                            row_factors(a - 2)

                steps(dve, step, first=-2)

            @block.gpsimd
            def _(pool):
                def add_rows(b, t, par):
                    pool.wait_ge(attn_ready, b * 8 + (5 + t))
                    pool.wait_ge(x_loaded, b * DMA + DMA)
                    pool.tensor_tensor(attn[par][:, t, :], attn[par][:, t, :], x_rows[:, t, :], ALU.add
                                       ).then_inc(resid_done, 1)

                def scale_rows(b, t, par):
                    pool.wait_ge(normed, b * 4 + (t + 1))
                    if t == 0:
                        at_least(pool, out_stored[par], b * (DMA * TT // 2) - par * (DMA * TT // 2))
                    pool.tensor_tensor(y[par][:, t, :], attn[par][:, t, :], gamma_all[:], ALU.mult
                                       ).then_inc(scaled, 1)
                    pool.wait_ge(scaled, b * 4 + (t + 1))
                    pool.tensor_tensor(y[par][:, t, :], y[par][:, t, :], beta_all[:], ALU.add).then_inc(out_ready, 1)

                def row_factors(b):
                    pool.wait_ge(var_ready, b * 2 + 2)
                    pool.tensor_tensor(rstd[:], var_eps[:], minus_half[:], ALU.pow).then_inc(rstd_ready, 1)
                    pool.wait_ge(rstd_ready, b + 1)
                    pool.tensor_tensor(shift[:], neg_mean[:], rstd[:], ALU.mult).then_inc(shift_ready, 1)

                pool.memset(minus_half[:], -0.5).then_inc(half_set, 1)
                pool.wait_ge(half_set, 1)

                def subtract_max(b, h, t):
                    u = 4 * h + t
                    pool.wait_ge(max_ready, b * 8 + (u + 1))
                    v = probs[h][:, t, :].rearrange("p (h s) -> p h s", h=HH)
                    pool.tensor_tensor(v, v, row_max[:, u, :].unsqueeze(2).broadcast_to([P, HH, S]),
                                       ALU.subtract).then_inc(shifted, 1)

                def step(a, par):
                    for s in range(8):
                        if s == 0:
                            if real(a - 1):
                                subtract_max(a - 1, 1, 3)
                        elif real(a):
                            subtract_max(a, (s - 1) // 4, (s - 1) % 4)
                        if s == 0 and real(a - 2):
                            add_rows(a - 2, 3, par)
                        if s >= 5 and real(a - 1):
                            add_rows(a - 1, s - 5, 1 - par)
                        if s == 2 and real(a - 2):
                            row_factors(a - 2)
                        if s in (1, 3) and real(a - 3):
                            scale_rows(a - 3, (s + 3) // 2, 1 - par)
                        if s in (4, 7) and real(a - 2):
                            scale_rows(a - 2, s // 7, par)

                steps(pool, step)

            @block.scalar
            def _(act):
                def exponent(b, h, t):
                    act.wait_ge(shifted, b * 8 + (4 * h + t + 1))
                    act.activation(probs[h][:, t, :], probs[h][:, t, :], ACT.Exp).then_inc(exp_done, 1)

                def high_x(b, k, par):
                    if k == 0:
                        act.wait_ge(xT_loaded, b * DMA + DMA)
                        at_least(act, q_done, b * 4 - 4)
                    act.copy(x_hi[par][:, k, :], xT_raw[:, k, :]).then_inc(x_hi_ready, 1)

                def high_keys(b, q, par):
                    rows = slice(DH * q, DH * q + DH)
                    if q == 0:
                        act.wait_ge(k_loaded, b * DMA + DMA)
                        at_least(act, scores_done, b * 8 - 8)
                        if isinstance(b, int) and b < 2:
                            act.wait_ge(zeros_set, 6)
                    act.copy(bd_hi[par][rows, :, q, :], k_raw[rows, :, :]).then_inc(bd_hi_ready, 1)

                def high_q(b, g):
                    act.wait_ge(q_done, b * 4 + (g + 1))
                    act.activation(q_hi[:, g, :], q_ps[:, :], ACT.Identity, bias=bq_col[:, g:g + 1]
                                   ).then_inc(q_hi_ready, 1)

                def copy_pt(b, h, i):
                    act.wait_ge(turned, b * (2 * NT) + (NT * h + i + 1))
                    w = tile_rows[i]
                    act.copy(pt[h][0:w, i, :], t_ps[(NT * h + i) % 2][0:w, :]).then_inc(pt_ready, 1)

                def norm(b, t, par):
                    act.wait_ge(shift_ready, b + 1)
                    act.activation(attn[par][:, t, :], attn[par][:, t, :], ACT.Identity,
                                   bias=shift[:, t:t + 1], scale=rstd[:, t:t + 1]).then_inc(normed, 1)

                def step(a, par):
                    for s in range(8):
                        h, t = s // 4, s % 4
                        if h == 1 and real(a + 2):
                            high_x(a + 2, t, par)
                        if h == 0 and real(a + 1):
                            high_keys(a + 1, t, 1 - par)
                        if t % 2 == 1 and real(a + h):
                            high_q(a + h, (2 if h == 0 else 0) + t // 2)
                        if s == 0:
                            if real(a - 1):
                                exponent(a - 1, 1, 3)
                        elif real(a):
                            exponent(a, (s - 1) // 4, (s - 1) % 4)
                        if real(a - 1 + h):
                            for i in ([], [0, 1], [2, 3], [4])[t]:
                                copy_pt(a - 1 + h, 1 - h, i)
                        if 3 <= s <= 6 and real(a - 2):
                            norm(a - 2, s - 3, par)

                steps(act, step, first=-2)


def kernel(x, ctx_1024, mask_BxS2_ik0, L0_xattn_edge_fea, L0_xattn_wq, L0_xattn_bq, L0_xattn_wk,
           L0_xattn_bk, L0_xattn_wv, L0_xattn_bv, L0_xattn_gamma, L0_xattn_beta):
    import numpy as np
    import concourse.bacc as bacc
    from concourse.bass_utils import run_bass_kernel_spmd

    c = np.ascontiguousarray
    B, T, D = x.shape
    S = ctx_1024.shape[1]
    assert B == 2 * HEADS

    def in_turns(a):
        a = np.asarray(a)
        return a.reshape(2, B // 2, *a.shape[1:]).swapaxes(0, 1).reshape(a.shape)

    x = in_turns(x)
    ctx = in_turns(ctx_1024)
    arrays = {
        "x": c(x),
        "xT": c(x.transpose(0, 2, 1)),
        "ctxT": c(ctx.reshape(B * S, D).T.reshape(D, B // 4, 4 * S)),
        "mask": c(np.asarray(mask_BxS2_ik0).reshape(HEADS, 2, S).swapaxes(0, 1).reshape(2, HEADS * S)),
        "wqT": c(np.asarray(L0_xattn_wq).T),
        "bq": c(np.asarray(L0_xattn_bq).reshape(D // 128, 128).T),
        "wkT": c(np.asarray(L0_xattn_wk).T),
        "bk": c(np.asarray(L0_xattn_bk).reshape(D // 128, 128).T),
        "wvT": c(np.asarray(L0_xattn_wv).T),
        "bv": c(np.asarray(L0_xattn_bv)),
        "gamma": c(np.asarray(L0_xattn_gamma)),
        "beta": c(np.asarray(L0_xattn_beta)),
    }
    nc = bacc.Bacc("TRN2", target_bir_lowering=False, num_devices=1)
    args = [nc.dram_tensor(f"in_{n}", a.shape, mybir.dt.from_np(a.dtype), kind="ExternalInput").ap()
            for n, a in arrays.items()]
    args.append(nc.dram_tensor("out_0", (B, T, D), F32, kind="ExternalOutput").ap())
    xattn(nc, *args)
    r = run_bass_kernel_spmd(nc, [{f"in_{n}": a for n, a in arrays.items()}], core_ids=[0])
    out = r.results[0]["out_0"]
    return c(out.reshape(B // 2, 2, T, D).swapaxes(0, 1).reshape(B, T, D))
```

```python
from contextlib import ExitStack

import concourse.bass as bass
from concourse import mybir

F32 = mybir.dt.float32
F32R = mybir.dt.float32r
I32 = mybir.dt.int32
ALU = mybir.AluOpType
ACT = mybir.ActivationFunctionType
AX = mybir.AxisListType

P = 128
HEADS = 16
PAD = float(-2**32 + 1)
LN_EPS = 1e-5
BANK = 512
DMA = 16


def at_least(eng, sem, value):
    if isinstance(value, int) and value <= 0:
        return
    eng.wait_ge(sem, value)


def xattn(nc, x, xT, ctxT, mask, wqT, bq, wkT, bk, wvT, bv, gamma, beta, out):
    B, T, D = x.shape
    S = mask.shape[1] // HEADS
    DH = D // HEADS
    KC = D // P
    NG = D // P
    HG = HEADS // NG
    TT = T // P
    HH = HEADS // 2
    ROWS = HH * S
    NT = -(-ROWS // P)
    VW = DH + 1
    SCALE = float(DH) ** -0.5
    GS = HG * S
    CB = 8
    CR = CB * S
    CHUNKS = B // CB
    HB = CB // 2
    HR = HB * S
    VT = -(-CR // P)
    v_n = [min(P, CR - P * j) for j in range(VT)]
    assert HR <= BANK and D == 512 and T == 512 and B % CB == 0

    tile_rows = [min(P, ROWS - P * i) for i in range(NT)]
    first_head = [P * i // S for i in range(NT)]
    last_head = [(P * i + tile_rows[i] - 1) // S for i in range(NT)]
    tile_cols = [(last_head[i] - first_head[i] + 1) * VW for i in range(NT)]
    VCOLS = max(tile_cols)
    pieces = []
    for i in range(NT):
        for hd in range(first_head[i], last_head[i] + 1):
            lo, hi = max(P * i, hd * S), min(P * i + tile_rows[i], (hd + 1) * S)
            pieces.append((i, lo - P * i, hd, lo - hd * S, hi - lo))

    k_dram = nc.dram_tensor("k_scratch", (B, P, NG, S), F32, kind="Internal").ap()
    v_dram = nc.dram_tensor("v_scratch", (B * S, HEADS * VW), F32, kind="Internal").ap()
    v_rows = v_dram.rearrange("(b s) (h w) -> b s h w", s=S, w=VW)

    with ExitStack() as whole:
        def sb(where, name, shape, dt):
            return where.enter_context(nc.sbuf_tensor(name, shape, dt))

        def ps(where, name, shape):
            return where.enter_context(nc.psum_tensor(name, shape, F32))

        def sem(name):
            return whole.enter_context(nc.semaphore(name))

        wq_hi = sb(whole, "wq_hi", [P, KC, D], F32R)
        wq_lo = sb(whole, "wq_lo", [P, KC, D], F32R)
        bq_col = sb(whole, "bq_col", [P, NG], F32)
        gamma_all = sb(whole, "gamma_all", [P, D], F32)
        beta_all = sb(whole, "beta_all", [P, D], F32)
        ident = sb(whole, "ident", [P, P], F32)
        mask_pad = [sb(whole, f"mask_pad{i}", [P, HEADS * S], F32) for i in range(2)]

        xT_raw = sb(whole, "xT_raw", [P, KC, T], F32)
        x_hi0 = sb(whole, "x_hi0", [P, KC, T], F32R)
        x_lo0 = sb(whole, "x_lo0", [P, KC, T], F32R)
        xT_loaded = sem("xT_loaded")
        x_hi_ready = sem("x_hi_ready")
        x_lo_ready = sem("x_lo_ready")

        start_loaded = [sem(f"start_loaded_{k}") for k in range(KC)]
        start_hi_ready = sem("start_hi_ready")
        start_lo_ready = sem("start_lo_ready")
        wv_loaded = sem("wv_loaded")
        wv_hi_ready = sem("wv_hi_ready")
        wv_lo_ready = sem("wv_lo_ready")
        wq_loaded = sem("wq_loaded")
        wq_hi_ready = sem("wq_hi_ready")
        wq_lo_ready = sem("wq_lo_ready")
        bk_loaded = sem("bk_loaded")
        bk_scaled = sem("bk_scaled")
        bv_loaded = sem("bv_loaded")
        consts_loaded = sem("consts_loaded")
        ones_set = sem("ones_set")
        ident_zero = sem("ident_zero")
        ident_set = sem("ident_set")
        ctx_loaded = sem("ctx_loaded")
        mask_loaded = sem("mask_loaded")
        mask_ready = sem("mask_ready")
        ctx_hi_ready = sem("ctx_hi_ready")
        ctx_lo_ready = sem("ctx_lo_ready")
        k_done = sem("k_done")
        k_copied = sem("k_copied")
        v_done = sem("v_done")
        v_copied = sem("v_copied")
        k_stored = [sem(f"k_stored_{i}") for i in range(2)]
        v_stored = sem("v_stored")

        with ExitStack() as one:
            wk_raw = sb(one, "wk_raw", [P, KC, D], F32)
            wv_raw = sb(one, "wv_raw", [P, KC, D], F32)
            wk_hi = sb(one, "wk_hi", [P, KC, D], F32R)
            wk_lo = sb(one, "wk_lo", [P, KC, D], F32R)
            wv_hi = sb(one, "wv_hi", [P, KC, D], F32R)
            wv_lo = sb(one, "wv_lo", [P, KC, D], F32R)
            mask_raw = sb(one, "mask_raw", [P, 2, HEADS * S], I32)
            bk_col = sb(one, "bk_col", [P, NG], F32)
            bk_sc = sb(one, "bk_sc", [P, NG], F32)
            bv_all = sb(one, "bv_all", [P, D], F32)
            ctx_raw = sb(one, "ctx_raw", [P, KC, CR], F32)
            ctx_hi = [sb(one, f"ctx_hi{i}", [P, KC, CR], F32R) for i in range(2)]
            ctx_lo = [sb(one, f"ctx_lo{i}", [P, KC, CR], F32R) for i in range(2)]
            k_out = sb(one, "k_out", [P, CB, NG, S], F32)
            v_out = sb(one, "v_out", [P, VT, HEADS, VW], F32)
            k_ps = [ps(one, f"k_ps{i}", [P, BANK]) for i in range(NG)]
            v_ps = [ps(one, f"v_ps{i}", [P, BANK]) for i in range(4)]

            block = one.enter_context(nc.Block())

            @block.sync
            def _(sp):
                wk_src = wkT.rearrange("(k p) n -> p k n", p=P)
                ctx_src = ctxT.rearrange("(k p) c r -> p k c r", p=P)
                for k in range(KC):
                    sp.dma_start(wk_raw[:, k, :], wk_src[:, k, :]).then_inc(start_loaded[k], DMA)
                    sp.dma_start(ctx_raw[:, k, 0:HR], ctx_src[:, k, 0, 0:HR]).then_inc(start_loaded[k], DMA)
                sp.dma_start(bk_col[:], bk).then_inc(bk_loaded, DMA)
                sp.dma_start(ctx_raw[:, :, HR:CR], ctx_src[:, :, 0, HR:CR]).then_inc(ctx_loaded, DMA)
                sp.dma_start(wv_raw[:], wvT.rearrange("(k p) n -> p k n", p=P)).then_inc(wv_loaded, DMA)
                sp.dma_start(bv_all[:], bv.partition_broadcast(P)).then_inc(bv_loaded, DMA)

                def load(c):
                    sp.wait_ge(ctx_hi_ready, c)
                    sp.wait_ge(ctx_lo_ready, c)
                    sp.dma_start(ctx_raw[:], ctx_src[:, :, c, :]).then_inc(ctx_loaded, DMA)

                def store_keys(c, half):
                    sp.wait_ge(k_copied, c * 2 * NG + (half + 1) * NG)
                    sp.dma_start(k_dram[c * CB + half * HB:c * CB + half * HB + HB].rearrange("b p m s -> p b (m s)"),
                                 k_out[:, half * HB:half * HB + HB, :, :].rearrange("p b m s -> p b (m s)")
                                 ).then_inc(k_stored[half], DMA)

                def store_values(c):
                    for j in range(VT):
                        sp.wait_ge(v_copied, c * VT + j + 1)
                        sp.dma_start(v_dram[c * CR + P * j:c * CR + P * j + v_n[j], :],
                                     v_out[0:v_n[j], j, :, :].rearrange("p h w -> p (h w)")
                                     ).then_inc(v_stored, DMA)

                sp.wait_ge(start_hi_ready, 2 * KC)
                sp.wait_ge(start_lo_ready, 2 * KC)
                load(1)
                sp.dma_start(wk_raw[:], wqT.rearrange("(k p) n -> p k n", p=P)).then_inc(wq_loaded, DMA)
                sp.dma_start(bq_col[:], bq).then_inc(consts_loaded, DMA)
                sp.dma_start(gamma_all[:], gamma.partition_broadcast(P)).then_inc(consts_loaded, DMA)
                sp.dma_start(beta_all[:], beta.partition_broadcast(P)).then_inc(consts_loaded, DMA)
                sp.dma_start(mask_raw[:], mask.partition_broadcast(P)).then_inc(mask_loaded, DMA)
                for c in range(CHUNKS):
                    store_keys(c, 0)
                    if 1 < c + 1 < CHUNKS:
                        load(c + 1)
                    store_keys(c, 1)
                    if c == 0:
                        sp.dma_start(xT_raw[:], xT[0].rearrange("(k p) t -> p k t", p=P)
                                     ).then_inc(xT_loaded, DMA)
                    store_values(c)
                sp.wait_ge(consts_loaded, 3 * DMA)
                for half in range(2):
                    sp.wait_ge(k_stored[half], DMA * CHUNKS)
                sp.wait_ge(v_stored, DMA * VT * CHUNKS)

            @block.gpsimd
            def _(pool):
                pool.memset(ident[:], 0.0).then_inc(ident_zero, 1)
                pool.wait_ge(ident_zero, 1)
                pool.affine_select(out=ident[:], in_=ident[:], compare_op=ALU.not_equal, fill=1.0,
                                   base=0, pattern=[[-1, P]], channel_multiplier=1).then_inc(ident_set, 1)
                pool.memset(v_out[:, :, :, DH:VW], 1.0).then_inc(ones_set, 1)
                pool.wait_ge(wq_hi_ready, 1)
                pool.tensor_tensor(wq_lo[:], wk_raw[:], wq_hi[:], ALU.subtract).then_inc(wq_lo_ready, 1)
                pool.wait_ge(mask_loaded, DMA)
                for i in range(2):
                    pool.tensor_scalar(mask_pad[i][:], mask_raw[:, i, :], PAD, None, ALU.mult
                                       ).then_inc(mask_ready, 1)
                pool.wait_ge(x_hi_ready, KC)
                for k in range(KC):
                    pool.tensor_tensor(x_lo0[:, k, :], xT_raw[:, k, :], x_hi0[:, k, :], ALU.subtract
                                       ).then_inc(x_lo_ready, 1)
                pool.wait_ge(ident_set, 1)
                pool.wait_ge(wq_lo_ready, 1)
                pool.wait_ge(mask_ready, 2)
                pool.wait_ge(x_lo_ready, KC)

            @block.scalar
            def _(act):
                def high(c):
                    act.wait_ge(ctx_loaded, (c + 1) * DMA)
                    at_least(act, k_done, (c - 1) * 2 * NG)
                    at_least(act, v_done, (c - 1) * VT)
                    first = HR if c == 0 else 0
                    act.copy(ctx_hi[c % 2][:, :, first:CR], ctx_raw[:, :, first:CR]).then_inc(ctx_hi_ready, 1)

                def keys(c, half):
                    at_least(act, k_stored[half], DMA * c)
                    for m in range(NG):
                        act.wait_ge(k_done, (2 * c + half) * NG + m + 1)
                        act.activation(k_out[:, half * HB:half * HB + HB, m, :],
                                       k_ps[m][:, 0:HR].rearrange("p (b s) -> p b s", b=HB), ACT.Identity,
                                       bias=bk_sc[:, m:m + 1], scale=SCALE).then_inc(k_copied, 1)

                for k in range(KC):
                    act.wait_ge(start_loaded[k], 2 * DMA)
                    act.copy(wk_hi[:, k, :], wk_raw[:, k, :]).then_inc(start_hi_ready, 1)
                    act.copy(ctx_hi[0][:, k, 0:HR], ctx_raw[:, k, 0:HR]).then_inc(start_hi_ready, 1)
                high(0)
                act.wait_ge(wv_loaded, DMA)
                act.copy(wv_hi[:], wv_raw[:]).then_inc(wv_hi_ready, 1)
                act.wait_ge(bk_scaled, 1)
                for c in range(CHUNKS):
                    keys(c, 0)
                    if c + 1 < CHUNKS:
                        high(c + 1)
                    keys(c, 1)
                    if c == 0:
                        act.wait_ge(wq_loaded, DMA)
                        act.copy(wq_hi[:], wk_raw[:]).then_inc(wq_hi_ready, 1)
                    if c == 1:
                        act.wait_ge(xT_loaded, DMA)
                        for k in range(KC):
                            act.copy(x_hi0[:, k, :], xT_raw[:, k, :]).then_inc(x_hi_ready, 1)

            @block.vector
            def _(dve):
                def low(c):
                    first = HR if c == 0 else 0
                    dve.wait_ge(ctx_hi_ready, c + 1)
                    dve.tensor_tensor(ctx_lo[c % 2][:, :, first:CR], ctx_raw[:, :, first:CR],
                                      ctx_hi[c % 2][:, :, first:CR], ALU.subtract).then_inc(ctx_lo_ready, 1)

                def values(c):
                    at_least(dve, v_stored, DMA * VT * c)
                    for j in range(VT):
                        n = v_n[j]
                        dve.wait_ge(v_done, c * VT + j + 1)
                        dve.tensor_tensor(v_out[0:n, j, :, 0:DH],
                                          v_ps[(c * VT + j) % 4][0:n, :].rearrange("p (h w) -> p h w", h=HEADS),
                                          bv_all[0:n, :].rearrange("p (h w) -> p h w", h=HEADS),
                                          ALU.add).then_inc(v_copied, 1)

                for k in range(KC):
                    dve.wait_ge(start_hi_ready, 2 * k + 1)
                    dve.tensor_tensor(wk_lo[:, k, :], wk_raw[:, k, :], wk_hi[:, k, :], ALU.subtract
                                      ).then_inc(start_lo_ready, 1)
                    dve.wait_ge(start_hi_ready, 2 * k + 2)
                    dve.tensor_tensor(ctx_lo[0][:, k, 0:HR], ctx_raw[:, k, 0:HR], ctx_hi[0][:, k, 0:HR],
                                      ALU.subtract).then_inc(start_lo_ready, 1)
                dve.wait_ge(bk_loaded, DMA)
                dve.tensor_scalar(bk_sc[:], bk_col[:], SCALE, None, ALU.mult).then_inc(bk_scaled, 1)
                low(0)
                dve.wait_ge(wv_hi_ready, 1)
                dve.tensor_tensor(wv_lo[:], wv_raw[:], wv_hi[:], ALU.subtract).then_inc(wv_lo_ready, 1)
                dve.wait_ge(bv_loaded, DMA)
                dve.wait_ge(ones_set, 1)
                for c in range(CHUNKS):
                    if c + 1 < CHUNKS:
                        low(c + 1)
                    values(c)

            @block.tensor
            def _(pe):
                terms = [(0, 1), (1, 0), (0, 0)]

                def key_products(c, half, m, k):
                    ctx_part = (ctx_hi[c % 2], ctx_lo[c % 2])
                    for n, (a, b) in enumerate(terms):
                        mm = pe.matmul(k_ps[m][:, 0:HR], (wk_hi, wk_lo)[a][:, k, P * m:P * m + P],
                                       ctx_part[b][:, k, half * HR:half * HR + HR],
                                       start=(k == 0 and n == 0), stop=(k == KC - 1 and n == 2))
                    if k == KC - 1:
                        mm.then_inc(k_done, 1)

                for k in range(KC):
                    pe.wait_ge(start_hi_ready, 2 * k + 2)
                    pe.wait_ge(start_lo_ready, 2 * k + 2)
                    for m in range(NG):
                        key_products(0, 0, m, k)
                for c in range(CHUNKS):
                    pe.wait_ge(ctx_hi_ready, c + 1)
                    pe.wait_ge(ctx_lo_ready, c + 1)
                    for half in range(1 if c == 0 else 0, 2):
                        for m in range(NG):
                            pe.wait_ge(k_copied, (2 * c + half - 1) * NG + m + 1)
                            for k in range(KC):
                                key_products(c, half, m, k)
                    if c == 0:
                        pe.wait_ge(wv_hi_ready, 1)
                        pe.wait_ge(wv_lo_ready, 1)
                    ctx_part = (ctx_hi[c % 2], ctx_lo[c % 2])
                    for j in range(VT):
                        at_least(pe, v_copied, c * VT + j - 3)
                        for k in range(KC):
                            for n, (a, b) in enumerate(terms):
                                mm = pe.matmul(v_ps[(c * VT + j) % 4][0:v_n[j], :],
                                               ctx_part[a][:, k, P * j:P * j + v_n[j]],
                                               (wv_hi, wv_lo)[b][:, k, :], start=(k == 0 and n == 0),
                                               stop=(k == KC - 1 and n == 2))
                        mm.then_inc(v_done, 1)

        k_loaded = sem("k_loaded")
        v_loaded = [sem(f"v_loaded_{h}") for h in range(2)]
        x_loaded = sem("x_loaded")
        out_stored = [sem(f"out_stored_{i}") for i in range(2)]
        q_done = sem("q_done")
        q_hi_ready = sem("q_hi_ready")
        q_lo_ready = sem("q_lo_ready")
        zeros_set = sem("zeros_set")
        bd_hi_ready = sem("bd_hi_ready")
        bd_lo_ready = sem("bd_lo_ready")
        scores_done = sem("scores_done")
        masked = sem("masked")
        max_ready = sem("max_ready")
        shifted = sem("shifted")
        exp_done = sem("exp_done")
        turned = sem("turned")
        pt_ready = sem("pt_ready")
        pv_done = sem("pv_done")
        inv_ready = sem("inv_ready")
        attn_ready = sem("attn_ready")
        resid_done = sem("resid_done")
        stats_done = sem("stats_done")
        meanvar_done = sem("meanvar_done")
        var_ready = sem("var_ready")
        half_set = sem("half_set")
        rstd_ready = sem("rstd_ready")
        shift_ready = sem("shift_ready")
        normed = sem("normed")
        scaled = sem("scaled")
        out_ready = sem("out_ready")

        with ExitStack() as two:
            x_hi = [x_hi0, sb(two, "x_hi1", [P, KC, T], F32R)]
            x_lo = [x_lo0, sb(two, "x_lo1", [P, KC, T], F32R)]
            q_hi = sb(two, "q_hi", [P, NG, T], F32R)
            q_lo = sb(two, "q_lo", [P, NG, T], F32R)
            k_raw = sb(two, "k_raw", [P, NG, S], F32)
            bd_hi = [sb(two, f"bd_hi{i}", [P, NG, HG, S], F32R) for i in range(2)]
            bd_lo = [sb(two, f"bd_lo{i}", [P, NG, HG, S], F32R) for i in range(2)]
            probs = [sb(two, f"probs{h}", [P, TT, ROWS], F32) for h in range(2)]
            row_max = sb(two, "row_max", [P, 2 * TT, HH], F32)
            pt = [sb(two, f"pt{h}", [P, NT, T], F32) for h in range(2)]
            v_tiles = [sb(two, f"v_tiles{h}", [P, NT, VCOLS], F32) for h in range(2)]
            inv_sum = sb(two, "inv_sum", [P, 2 * TT, HH], F32)
            x_rows = sb(two, "x_rows", [P, TT, D], F32)
            attn = [sb(two, f"attn{i}", [P, TT, D], F32) for i in range(2)]
            y = [sb(two, f"y{i}", [P, TT, D], F32) for i in range(2)]
            stats = sb(two, "stats", [P, TT, 6], F32)
            meanvar = sb(two, "meanvar", [P, TT, 2], F32)
            var_eps = sb(two, "var_eps", [P, TT], F32)
            neg_mean = sb(two, "neg_mean", [P, TT], F32)
            minus_half = sb(two, "minus_half", [P, TT], F32)
            rstd = sb(two, "rstd", [P, TT], F32)
            shift = sb(two, "shift", [P, TT], F32)
            s_ps = [ps(two, f"s_ps{i}", [P, 2, BANK]) for i in range(2)]
            t_ps = [ps(two, f"t_ps{i}", [P, BANK]) for i in range(2)]
            q_ps = ps(two, "q_ps", [P, BANK])
            o_ps = ps(two, "o_ps", [P, BANK])

            def real(b):
                return not isinstance(b, int) or 0 <= b < B

            def steps(eng, body, first=-1):
                for a in range(first, 4):
                    body(a, a % 2)
                with eng.Fori(2, B // 2 - 1) as pair:
                    body(pair * 2, 0)
                    body(pair * 2 + 1, 1)
                for a in range(B - 2, B + 3):
                    body(a, a % 2)

            block = two.enter_context(nc.Block())

            @block.sync
            def _(sp):
                def load_v(b, h):
                    at_least(sp, pv_done, b * 8 + (4 * h - 4))
                    if isinstance(b, int) and b == 0:
                        sp.wait_ge(zeros_set, 6)
                    for i, row, hd, key, n in pieces:
                        col = (hd - first_head[i]) * VW
                        sp.dma_start(v_tiles[h][row:row + n, i, col:col + VW],
                                     v_rows[b, key:key + n, HH * h + hd, :]).then_inc(v_loaded[h], DMA)

                def store(b, t, par):
                    sp.wait_ge(out_ready, b * 4 + (t + 1))
                    sp.dma_start(out[b, P * t:P * t + P, :], y[par][:, t, :]).then_inc(out_stored[par], DMA)

                def step(a, par):
                    if real(a + 2) and not (isinstance(a, int) and a == -2):
                        at_least(sp, x_hi_ready, a * 4 + 8)
                        at_least(sp, x_lo_ready, a * 4 + 8)
                        sp.dma_start(xT_raw[:], xT[a + 2].rearrange("(k p) t -> p k t", p=P)
                                     ).then_inc(xT_loaded, DMA)
                    if real(a - 1):
                        load_v(a - 1, 1)
                        at_least(sp, resid_done, a * 4 - 4)
                        sp.dma_start(x_rows[:], x[a - 1].rearrange("(t p) d -> p t d", p=P)
                                     ).then_inc(x_loaded, DMA)
                    if real(a - 3):
                        store(a - 3, 2, 1 - par)
                        store(a - 3, 3, 1 - par)
                    if real(a):
                        load_v(a, 0)
                    if real(a - 2):
                        store(a - 2, 0, par)
                    if real(a + 2):
                        at_least(sp, bd_hi_ready, a * 4 + 8)
                        at_least(sp, bd_lo_ready, a * 4 + 8)
                        sp.dma_start(k_raw[:], k_dram[a + 2]).then_inc(k_loaded, DMA)
                    if real(a - 2):
                        store(a - 2, 1, par)

                steps(sp, step, first=-2)
                for par in range(2):
                    sp.wait_ge(out_stored[par], DMA * TT * B // 2)

            @block.tensor
            def _(pe):
                terms = [(0, 1), (1, 0), (0, 0)]

                def q_half(b, g, part, par):
                    if part == 0:
                        pe.wait_ge(x_hi_ready, b * 4 + 4)
                        pe.wait_ge(x_lo_ready, b * 4 + 4)
                        at_least(pe, q_hi_ready, b * 4 + g)
                        at_least(pe, q_lo_ready, b * 4 + g)
                    x_part = (x_hi[par], x_lo[par])
                    for k in (2 * part, 2 * part + 1):
                        for n, (u, v) in enumerate(terms):
                            mm = pe.matmul(q_ps[:, :], (wq_hi, wq_lo)[u][:, k, P * g:P * g + P],
                                           x_part[v][:, k, :], start=(k == 0 and n == 0),
                                           stop=(k == KC - 1 and n == 2))
                    if part == 1:
                        mm.then_inc(q_done, 1)

                def scores(b, h, t, par):
                    pe.wait_ge(q_hi_ready, b * 4 + (2 * h + 2))
                    pe.wait_ge(q_lo_ready, b * 4 + (2 * h + 2))
                    pe.wait_ge(bd_hi_ready, b * 4 + 4)
                    pe.wait_ge(bd_lo_ready, b * 4 + 4)
                    at_least(pe, masked, b * 8 + (4 * h + t - 1))
                    for j in range(2):
                        g = 2 * h + j
                        for n, (u, v) in enumerate(terms):
                            mm = pe.matmul(s_ps[t % 2][:, j, 0:GS], (q_hi, q_lo)[u][:, g, P * t:P * t + P],
                                           (bd_hi, bd_lo)[v][par][:, g, :, :].rearrange("p h s -> p (h s)"),
                                           start=(n == 0), stop=(n == 2))
                    mm.then_inc(scores_done, 1)

                def turn(b, h, i):
                    pe.wait_ge(exp_done, b * 8 + (4 * h + 4))
                    at_least(pe, pt_ready, b * (2 * NT) + (NT * h + i - 1))
                    w = tile_rows[i]
                    for t in range(TT):
                        mm = pe.transpose(t_ps[(NT * h + i) % 2][0:w, P * t:P * t + P],
                                          probs[h][:, t, P * i:P * i + w], ident[:, :])
                    mm.then_inc(turned, 1)

                def product(b, h, t):
                    pe.wait_ge(pt_ready, b * (2 * NT) + (NT * h + NT))
                    pe.wait_ge(v_loaded[h], (b + 1) * (DMA * len(pieces)))
                    at_least(pe, attn_ready, b * 8 + (4 * h + t))
                    for i in range(NT):
                        w, col = tile_rows[i], first_head[i] * VW
                        mm = pe.matmul(o_ps[:, col:col + tile_cols[i]], pt[h][0:w, i, P * t:P * t + P],
                                       v_tiles[h][0:w, i, 0:tile_cols[i]], start=(i == 0),
                                       stop=(i == NT - 1), skip_group_check=True)
                    mm.then_inc(pv_done, 1)

                def step(a, par):
                    for s in range(8):
                        h, t = s // 4, s % 4
                        qb = a + h
                        if real(qb):
                            q_half(qb, (2 if h == 0 else 0) + t // 2, t % 2, (par + h) % 2)
                        if real(a):
                            scores(a, h, t, par)
                        if real(a - 1 + h):
                            for i in ([], [0, 1], [2, 3], [4])[t]:
                                turn(a - 1 + h, 1 - h, i)
                        if real(a - 1):
                            product(a - 1, h, t)

                steps(pe, step)

            @block.vector
            def _(dve):
                o_heads = o_ps[:, 0:HH * VW].rearrange("p (h w) -> p h w", w=VW)
                dve.memset(bd_hi[0][:].bitcast(F32), 0.0).then_inc(zeros_set, 1)
                dve.memset(bd_hi[1][:].bitcast(F32), 0.0).then_inc(zeros_set, 1)

                def invert_sums(b, h, t):
                    u = 4 * h + t
                    dve.wait_ge(pv_done, b * 8 + (u + 1))
                    dve.reciprocal(inv_sum[:, u, :], o_heads[:, :, DH]).then_inc(inv_ready, 1)

                def scale_attn(b, h, t, par):
                    u = 4 * h + t
                    dve.wait_ge(inv_ready, b * 8 + (u + 1))
                    if h == 0:
                        at_least(dve, scaled, b * 4 + (t - 7))
                    dve.tensor_tensor(attn[par][:, t, HH * DH * h:HH * DH * (h + 1)].rearrange(
                                          "p (h w) -> p h w", w=DH),
                                      o_heads[:, :, 0:DH],
                                      inv_sum[:, u, :].unsqueeze(2).broadcast_to([P, HH, DH]),
                                      ALU.mult).then_inc(attn_ready, 1)

                def row_stats(b, t, par):
                    dve.wait_ge(resid_done, b * 4 + (t + 1))
                    dve.bn_stats(stats[:, t, :], attn[par][:, t, :]).then_inc(stats_done, 1)

                def mean_and_var(b, t):
                    dve.bn_aggr(meanvar[:, t, :], stats[:, t, :]).then_inc(meanvar_done, 1)

                def row_factors(b):
                    dve.wait_ge(meanvar_done, b * 4 + 4)
                    at_least(dve, normed, b * 4)
                    dve.tensor_scalar(var_eps[:], meanvar[:, :, 1], LN_EPS, None, ALU.add
                                      ).then_inc(var_ready, 1)
                    dve.tensor_scalar(neg_mean[:], meanvar[:, :, 0], -1.0, None, ALU.mult
                                      ).then_inc(var_ready, 1)

                def split_x(b, k, par):
                    dve.wait_ge(x_hi_ready, b * 4 + (k + 1))
                    dve.tensor_tensor(x_lo[par][:, k, :], xT_raw[:, k, :], x_hi[par][:, k, :], ALU.subtract
                                      ).then_inc(x_lo_ready, 1)

                def low_keys(b, q, par):
                    rows = slice(DH * q, DH * q + DH)
                    dve.wait_ge(bd_hi_ready, b * 4 + (q + 1))
                    dve.tensor_tensor(bd_lo[par][rows, :, q, :], k_raw[rows, :, :], bd_hi[par][rows, :, q, :],
                                      ALU.subtract).then_inc(bd_lo_ready, 1)

                def q_low(b, g):
                    dve.wait_ge(q_hi_ready, b * 4 + (g + 1))
                    dve.scalar_tensor_tensor(out=q_lo[:, g, :], in0=q_ps[:, :], scalar=bq_col[:, g:g + 1],
                                             in1=q_hi[:, g, :], op0=ALU.add, op1=ALU.subtract
                                             ).then_inc(q_lo_ready, 1)

                def add_mask(b, h, t, par):
                    u = 4 * h + t
                    dve.wait_ge(scores_done, b * 8 + (u + 1))
                    if t == 0:
                        at_least(dve, turned, b * (2 * NT) + (NT * h - NT))
                    dve.tensor_tensor(probs[h][:, t, :].rearrange("p (j c) -> p j c", j=2),
                                      s_ps[t % 2][:, :, 0:GS],
                                      mask_pad[par][:, ROWS * h:ROWS * h + ROWS].rearrange("p (j c) -> p j c", j=2),
                                      ALU.add).then_inc(masked, 1)

                def maximum(b, h, t):
                    u = 4 * h + t
                    dve.wait_ge(masked, b * 8 + (u + 1))
                    dve.tensor_reduce(row_max[:, u, :], probs[h][:, t, :].rearrange("p (h s) -> p h s", h=HH),
                                      AX.X, ALU.max).then_inc(max_ready, 1)

                def step(a, par):
                    for s in range(8):
                        h, t = s // 4, s % 4
                        last = None
                        if s == 0 and real(a - 2):
                            last = (a - 2, 1, 3)
                        if s > 0 and real(a - 1):
                            last = (a - 1, (s - 1) // 4, (s - 1) % 4)
                        if last is not None:
                            invert_sums(*last)
                        if 1 <= s <= 4 and real(a + 1):
                            low_keys(a + 1, s - 1, 1 - par)
                        if last is not None:
                            scale_attn(*last, par if s == 0 else 1 - par)
                        rows = None
                        if real(a - 2) and s < 2:
                            rows = (a - 2, 2 + s)
                            row_stats(*rows, par)
                        if real(a - 1) and s >= 6:
                            rows = (a - 1, s - 6)
                            row_stats(*rows, 1 - par)
                        if s == 3 and real(a + 2):
                            split_x(a + 2, 0, par)
                        if real(a + h) and t % 2 == 1:
                            q_low(a + h, (2 if h == 0 else 0) + t // 2)
                        if real(a):
                            add_mask(a, h, t, par)
                        if 4 <= s <= 6 and real(a + 2):
                            split_x(a + 2, s - 3, par)
                        if rows is not None:
                            dve.wait_ge(stats_done, rows[0] * 4 + (rows[1] + 1))
                        if real(a):
                            maximum(a, h, t)
                        if rows is not None:
                            mean_and_var(*rows)
                        if s == 1 and real(a - 2):
                            row_factors(a - 2)

                steps(dve, step)

            @block.gpsimd
            def _(pool):
                def add_rows(b, t, par):
                    pool.wait_ge(attn_ready, b * 8 + (5 + t))
                    pool.wait_ge(x_loaded, b * DMA + DMA)
                    pool.tensor_tensor(attn[par][:, t, :], attn[par][:, t, :], x_rows[:, t, :], ALU.add
                                       ).then_inc(resid_done, 1)

                def scale_rows(b, t, par):
                    pool.wait_ge(normed, b * 4 + (t + 1))
                    if t == 0:
                        at_least(pool, out_stored[par], b * (DMA * TT // 2) - par * (DMA * TT // 2))
                    pool.tensor_tensor(y[par][:, t, :], attn[par][:, t, :], gamma_all[:], ALU.mult
                                       ).then_inc(scaled, 1)
                    pool.wait_ge(scaled, b * 4 + (t + 1))
                    pool.tensor_tensor(y[par][:, t, :], y[par][:, t, :], beta_all[:], ALU.add).then_inc(out_ready, 1)

                def row_factors(b):
                    pool.wait_ge(var_ready, b * 2 + 2)
                    pool.tensor_tensor(rstd[:], var_eps[:], minus_half[:], ALU.pow).then_inc(rstd_ready, 1)
                    pool.wait_ge(rstd_ready, b + 1)
                    pool.tensor_tensor(shift[:], neg_mean[:], rstd[:], ALU.mult).then_inc(shift_ready, 1)

                pool.memset(bd_lo[0][:].bitcast(F32), 0.0).then_inc(zeros_set, 1)
                pool.memset(bd_lo[1][:].bitcast(F32), 0.0).then_inc(zeros_set, 1)
                pool.memset(v_tiles[0][:], 0.0).then_inc(zeros_set, 1)
                pool.memset(v_tiles[1][:], 0.0).then_inc(zeros_set, 1)
                pool.memset(minus_half[:], -0.5).then_inc(half_set, 1)
                pool.wait_ge(half_set, 1)

                def subtract_max(b, h, t):
                    u = 4 * h + t
                    pool.wait_ge(max_ready, b * 8 + (u + 1))
                    v = probs[h][:, t, :].rearrange("p (h s) -> p h s", h=HH)
                    pool.tensor_tensor(v, v, row_max[:, u, :].unsqueeze(2).broadcast_to([P, HH, S]),
                                       ALU.subtract).then_inc(shifted, 1)

                def step(a, par):
                    for s in range(8):
                        if s == 0:
                            if real(a - 1):
                                subtract_max(a - 1, 1, 3)
                        elif real(a):
                            subtract_max(a, (s - 1) // 4, (s - 1) % 4)
                        if s == 0 and real(a - 2):
                            add_rows(a - 2, 3, par)
                        if s >= 5 and real(a - 1):
                            add_rows(a - 1, s - 5, 1 - par)
                        if s == 2 and real(a - 2):
                            row_factors(a - 2)
                        if s in (1, 3) and real(a - 3):
                            scale_rows(a - 3, (s + 3) // 2, 1 - par)
                        if s in (4, 7) and real(a - 2):
                            scale_rows(a - 2, s // 7, par)

                steps(pool, step)

            @block.scalar
            def _(act):
                def exponent(b, h, t):
                    act.wait_ge(shifted, b * 8 + (4 * h + t + 1))
                    act.activation(probs[h][:, t, :], probs[h][:, t, :], ACT.Exp).then_inc(exp_done, 1)

                def high_x(b, k, par):
                    if k == 0:
                        act.wait_ge(xT_loaded, b * DMA + DMA)
                        at_least(act, scores_done, b * 8 - 13)
                    if k == 2:
                        at_least(act, q_done, b * 4 - 4)
                    act.copy(x_hi[par][:, k, :], xT_raw[:, k, :]).then_inc(x_hi_ready, 1)

                def high_keys(b, q, par):
                    rows = slice(DH * q, DH * q + DH)
                    if q == 0:
                        act.wait_ge(k_loaded, b * DMA + DMA)
                        at_least(act, scores_done, b * 8 - 8)
                        if isinstance(b, int) and b < 2:
                            act.wait_ge(zeros_set, 6)
                    act.copy(bd_hi[par][rows, :, q, :], k_raw[rows, :, :]).then_inc(bd_hi_ready, 1)

                def high_q(b, g):
                    act.wait_ge(q_done, b * 4 + (g + 1))
                    act.activation(q_hi[:, g, :], q_ps[:, :], ACT.Identity, bias=bq_col[:, g:g + 1]
                                   ).then_inc(q_hi_ready, 1)

                def copy_pt(b, h, i):
                    act.wait_ge(turned, b * (2 * NT) + (NT * h + i + 1))
                    w = tile_rows[i]
                    act.copy(pt[h][0:w, i, :], t_ps[(NT * h + i) % 2][0:w, :]).then_inc(pt_ready, 1)

                def norm(b, t, par):
                    act.wait_ge(shift_ready, b + 1)
                    act.activation(attn[par][:, t, :], attn[par][:, t, :], ACT.Identity,
                                   bias=shift[:, t:t + 1], scale=rstd[:, t:t + 1]).then_inc(normed, 1)

                def step(a, par):
                    for s in range(8):
                        h, t = s // 4, s % 4
                        if 3 <= s <= 6 and real(a + 2):
                            high_x(a + 2, s - 3, par)
                        if h == 0 and real(a + 1):
                            high_keys(a + 1, t, 1 - par)
                        if t % 2 == 1 and real(a + h):
                            high_q(a + h, (2 if h == 0 else 0) + t // 2)
                        if s == 0:
                            if real(a - 1):
                                exponent(a - 1, 1, 3)
                        elif real(a):
                            exponent(a, (s - 1) // 4, (s - 1) % 4)
                        if real(a - 1 + h):
                            for i in ([], [0, 1], [2, 3], [4])[t]:
                                copy_pt(a - 1 + h, 1 - h, i)
                        if 3 <= s <= 6 and real(a - 2):
                            norm(a - 2, s - 3, par)

                steps(act, step)


def kernel(x, ctx_1024, mask_BxS2_ik0, L0_xattn_edge_fea, L0_xattn_wq, L0_xattn_bq, L0_xattn_wk,
           L0_xattn_bk, L0_xattn_wv, L0_xattn_bv, L0_xattn_gamma, L0_xattn_beta):
    import numpy as np
    import concourse.bacc as bacc
    from concourse.bass_utils import run_bass_kernel_spmd

    c = np.ascontiguousarray
    B, T, D = x.shape
    S = ctx_1024.shape[1]
    assert B == 2 * HEADS

    def in_turns(a):
        a = np.asarray(a)
        return a.reshape(2, B // 2, *a.shape[1:]).swapaxes(0, 1).reshape(a.shape)

    x = in_turns(x)
    ctx = in_turns(ctx_1024)
    arrays = {
        "x": c(x),
        "xT": c(x.transpose(0, 2, 1)),
        "ctxT": c(ctx.reshape(B * S, D).T.reshape(D, B // 8, 8 * S)),
        "mask": c(np.asarray(mask_BxS2_ik0).reshape(HEADS, 2, S).swapaxes(0, 1).reshape(2, HEADS * S)),
        "wqT": c(np.asarray(L0_xattn_wq).T),
        "bq": c(np.asarray(L0_xattn_bq).reshape(D // 128, 128).T),
        "wkT": c(np.asarray(L0_xattn_wk).T),
        "bk": c(np.asarray(L0_xattn_bk).reshape(D // 128, 128).T),
        "wvT": c(np.asarray(L0_xattn_wv).T),
        "bv": c(np.asarray(L0_xattn_bv)),
        "gamma": c(np.asarray(L0_xattn_gamma)),
        "beta": c(np.asarray(L0_xattn_beta)),
    }
    nc = bacc.Bacc("TRN2", target_bir_lowering=False, num_devices=1)
    args = [nc.dram_tensor(f"in_{n}", a.shape, mybir.dt.from_np(a.dtype), kind="ExternalInput").ap()
            for n, a in arrays.items()]
    args.append(nc.dram_tensor("out_0", (B, T, D), F32, kind="ExternalOutput").ap())
    xattn(nc, *args)
    r = run_bass_kernel_spmd(nc, [{f"in_{n}": a for n, a in arrays.items()}], core_ids=[0])
    out = r.results[0]["out_0"]
    return c(out.reshape(B // 2, 2, T, D).swapaxes(0, 1).reshape(B, T, D))
```

```python
from contextlib import ExitStack

import concourse.bass as bass
from concourse import mybir

F32 = mybir.dt.float32
F32R = mybir.dt.float32r
I32 = mybir.dt.int32
ALU = mybir.AluOpType
ACT = mybir.ActivationFunctionType
AX = mybir.AxisListType

P = 128
HEADS = 16
PAD = float(-2**32 + 1)
LN_EPS = 1e-5
BANK = 512
DMA = 16


def at_least(eng, sem, value):
    if isinstance(value, int) and value <= 0:
        return
    eng.wait_ge(sem, value)


def xattn(nc, x, xT, ctxT, mask, wqT, bq, wkT, bk, wvT, bv, gamma, beta, out):
    B, T, D = x.shape
    S = mask.shape[1] // HEADS
    DH = D // HEADS
    KC = D // P
    NG = D // P
    HG = HEADS // NG
    TT = T // P
    HH = HEADS // 2
    ROWS = HH * S
    NT = -(-ROWS // P)
    VW = DH + 1
    SCALE = float(DH) ** -0.5
    GS = HG * S
    CB = 8
    CR = CB * S
    CHUNKS = B // CB
    HB = CB // 2
    HR = HB * S
    VT = -(-CR // P)
    v_n = [min(P, CR - P * j) for j in range(VT)]
    assert HR <= BANK and D == 512 and T == 512 and B % CB == 0

    tile_rows = [min(P, ROWS - P * i) for i in range(NT)]
    first_head = [P * i // S for i in range(NT)]
    last_head = [(P * i + tile_rows[i] - 1) // S for i in range(NT)]
    tile_cols = [(last_head[i] - first_head[i] + 1) * VW for i in range(NT)]
    VCOLS = max(tile_cols)
    pieces = []
    for i in range(NT):
        for hd in range(first_head[i], last_head[i] + 1):
            lo, hi = max(P * i, hd * S), min(P * i + tile_rows[i], (hd + 1) * S)
            pieces.append((i, lo - P * i, hd, lo - hd * S, hi - lo))

    k_dram = nc.dram_tensor("k_scratch", (B, P, NG, S), F32, kind="Internal").ap()
    v_dram = nc.dram_tensor("v_scratch", (B * S, HEADS * VW), F32, kind="Internal").ap()
    v_rows = v_dram.rearrange("(b s) (h w) -> b s h w", s=S, w=VW)

    with ExitStack() as whole:
        def sb(where, name, shape, dt):
            return where.enter_context(nc.sbuf_tensor(name, shape, dt))

        def ps(where, name, shape):
            return where.enter_context(nc.psum_tensor(name, shape, F32))

        def sem(name):
            return whole.enter_context(nc.semaphore(name))

        wq_hi = sb(whole, "wq_hi", [P, KC, D], F32R)
        wq_lo = sb(whole, "wq_lo", [P, KC, D], F32R)
        bq_col = sb(whole, "bq_col", [P, NG], F32)
        gamma_all = sb(whole, "gamma_all", [P, D], F32)
        beta_all = sb(whole, "beta_all", [P, D], F32)
        ident = sb(whole, "ident", [P, P], F32)
        mask_pad = [sb(whole, f"mask_pad{i}", [P, HEADS * S], F32) for i in range(2)]

        xT_raw = sb(whole, "xT_raw", [P, KC, T], F32)
        x_hi0 = sb(whole, "x_hi0", [P, KC, T], F32R)
        x_lo0 = sb(whole, "x_lo0", [P, KC, T], F32R)
        xT_loaded = sem("xT_loaded")
        x_hi_ready = sem("x_hi_ready")
        x_lo_ready = sem("x_lo_ready")

        start_loaded = [sem(f"start_loaded_{k}") for k in range(KC)]
        start_hi_ready = sem("start_hi_ready")
        start_lo_ready = sem("start_lo_ready")
        wv_loaded = sem("wv_loaded")
        wv_hi_ready = sem("wv_hi_ready")
        wv_lo_ready = sem("wv_lo_ready")
        wq_loaded = sem("wq_loaded")
        wq_hi_ready = sem("wq_hi_ready")
        wq_lo_ready = sem("wq_lo_ready")
        bk_loaded = sem("bk_loaded")
        bk_scaled = sem("bk_scaled")
        bv_loaded = sem("bv_loaded")
        consts_loaded = sem("consts_loaded")
        ones_set = sem("ones_set")
        ident_zero = sem("ident_zero")
        ident_set = sem("ident_set")
        ctx_loaded = sem("ctx_loaded")
        mask_loaded = sem("mask_loaded")
        mask_ready = sem("mask_ready")
        ctx_hi_ready = sem("ctx_hi_ready")
        ctx_lo_ready = sem("ctx_lo_ready")
        k_done = sem("k_done")
        k_copied = sem("k_copied")
        v_done = sem("v_done")
        v_copied = sem("v_copied")
        k_stored = [sem(f"k_stored_{i}") for i in range(2)]
        v_stored = sem("v_stored")

        with ExitStack() as one:
            wk_raw = sb(one, "wk_raw", [P, KC, D], F32)
            wv_raw = sb(one, "wv_raw", [P, KC, D], F32)
            wk_hi = sb(one, "wk_hi", [P, KC, D], F32R)
            wk_lo = sb(one, "wk_lo", [P, KC, D], F32R)
            wv_hi = sb(one, "wv_hi", [P, KC, D], F32R)
            wv_lo = sb(one, "wv_lo", [P, KC, D], F32R)
            mask_raw = sb(one, "mask_raw", [P, 2, HEADS * S], I32)
            bk_col = sb(one, "bk_col", [P, NG], F32)
            bk_sc = sb(one, "bk_sc", [P, NG], F32)
            bv_all = sb(one, "bv_all", [P, D], F32)
            ctx_raw = sb(one, "ctx_raw", [P, KC, CR], F32)
            ctx_hi = [sb(one, f"ctx_hi{i}", [P, KC, CR], F32R) for i in range(2)]
            ctx_lo = [sb(one, f"ctx_lo{i}", [P, KC, CR], F32R) for i in range(2)]
            k_out = sb(one, "k_out", [P, CB, NG, S], F32)
            v_out = sb(one, "v_out", [P, VT, HEADS, VW], F32)
            k_ps = [ps(one, f"k_ps{i}", [P, BANK]) for i in range(NG)]
            v_ps = [ps(one, f"v_ps{i}", [P, BANK]) for i in range(4)]

            block = one.enter_context(nc.Block())

            @block.sync
            def _(sp):
                wk_src = wkT.rearrange("(k p) n -> p k n", p=P)
                ctx_src = ctxT.rearrange("(k p) c r -> p k c r", p=P)
                for k in range(KC):
                    sp.dma_start(wk_raw[:, k, :], wk_src[:, k, :]).then_inc(start_loaded[k], DMA)
                    sp.dma_start(ctx_raw[:, k, 0:HR], ctx_src[:, k, 0, 0:HR]).then_inc(start_loaded[k], DMA)
                sp.dma_start(bk_col[:], bk).then_inc(bk_loaded, DMA)
                sp.dma_start(ctx_raw[:, :, HR:CR], ctx_src[:, :, 0, HR:CR]).then_inc(ctx_loaded, DMA)
                sp.dma_start(wv_raw[:], wvT.rearrange("(k p) n -> p k n", p=P)).then_inc(wv_loaded, DMA)
                sp.dma_start(bv_all[:], bv.partition_broadcast(P)).then_inc(bv_loaded, DMA)

                def load(c):
                    sp.wait_ge(ctx_hi_ready, c)
                    sp.wait_ge(ctx_lo_ready, c)
                    sp.dma_start(ctx_raw[:], ctx_src[:, :, c, :]).then_inc(ctx_loaded, DMA)

                def store_keys(c, half):
                    sp.wait_ge(k_copied, c * 2 * NG + (half + 1) * NG)
                    sp.dma_start(k_dram[c * CB + half * HB:c * CB + half * HB + HB].rearrange("b p m s -> p b (m s)"),
                                 k_out[:, half * HB:half * HB + HB, :, :].rearrange("p b m s -> p b (m s)")
                                 ).then_inc(k_stored[half], DMA)

                def store_values(c):
                    for j in range(VT):
                        sp.wait_ge(v_copied, c * VT + j + 1)
                        sp.dma_start(v_dram[c * CR + P * j:c * CR + P * j + v_n[j], :],
                                     v_out[0:v_n[j], j, :, :].rearrange("p h w -> p (h w)")
                                     ).then_inc(v_stored, DMA)

                sp.wait_ge(start_hi_ready, 2 * KC)
                sp.wait_ge(start_lo_ready, 2 * KC)
                load(1)
                sp.dma_start(wk_raw[:], wqT.rearrange("(k p) n -> p k n", p=P)).then_inc(wq_loaded, DMA)
                sp.dma_start(bq_col[:], bq).then_inc(consts_loaded, DMA)
                sp.dma_start(gamma_all[:], gamma.partition_broadcast(P)).then_inc(consts_loaded, DMA)
                sp.dma_start(beta_all[:], beta.partition_broadcast(P)).then_inc(consts_loaded, DMA)
                sp.dma_start(mask_raw[:], mask.partition_broadcast(P)).then_inc(mask_loaded, DMA)
                for c in range(CHUNKS):
                    store_keys(c, 0)
                    if 1 < c + 1 < CHUNKS:
                        load(c + 1)
                    store_keys(c, 1)
                    if c == 0:
                        sp.dma_start(xT_raw[:], xT[0].rearrange("(k p) t -> p k t", p=P)
                                     ).then_inc(xT_loaded, DMA)
                    store_values(c)
                sp.wait_ge(consts_loaded, 3 * DMA)
                for half in range(2):
                    sp.wait_ge(k_stored[half], DMA * CHUNKS)
                sp.wait_ge(v_stored, DMA * VT * CHUNKS)

            @block.gpsimd
            def _(pool):
                pool.memset(ident[:], 0.0).then_inc(ident_zero, 1)
                pool.wait_ge(ident_zero, 1)
                pool.affine_select(out=ident[:], in_=ident[:], compare_op=ALU.not_equal, fill=1.0,
                                   base=0, pattern=[[-1, P]], channel_multiplier=1).then_inc(ident_set, 1)
                pool.memset(v_out[:, :, :, DH:VW], 1.0).then_inc(ones_set, 1)
                pool.wait_ge(wq_hi_ready, 1)
                pool.tensor_tensor(wq_lo[:], wk_raw[:], wq_hi[:], ALU.subtract).then_inc(wq_lo_ready, 1)
                pool.wait_ge(mask_loaded, DMA)
                for i in range(2):
                    pool.tensor_scalar(mask_pad[i][:], mask_raw[:, i, :], PAD, None, ALU.mult
                                       ).then_inc(mask_ready, 1)
                pool.wait_ge(x_hi_ready, KC)
                for k in range(KC):
                    pool.tensor_tensor(x_lo0[:, k, :], xT_raw[:, k, :], x_hi0[:, k, :], ALU.subtract
                                       ).then_inc(x_lo_ready, 1)
                pool.wait_ge(ident_set, 1)
                pool.wait_ge(wq_lo_ready, 1)
                pool.wait_ge(mask_ready, 2)
                pool.wait_ge(x_lo_ready, KC)

            @block.scalar
            def _(act):
                def high(c):
                    act.wait_ge(ctx_loaded, (c + 1) * DMA)
                    at_least(act, k_done, (c - 1) * 2 * NG)
                    at_least(act, v_done, (c - 1) * VT)
                    first = HR if c == 0 else 0
                    act.copy(ctx_hi[c % 2][:, :, first:CR], ctx_raw[:, :, first:CR]).then_inc(ctx_hi_ready, 1)

                def keys(c, half):
                    at_least(act, k_stored[half], DMA * c)
                    for m in range(NG):
                        act.wait_ge(k_done, (2 * c + half) * NG + m + 1)
                        act.activation(k_out[:, half * HB:half * HB + HB, m, :],
                                       k_ps[m][:, 0:HR].rearrange("p (b s) -> p b s", b=HB), ACT.Identity,
                                       bias=bk_sc[:, m:m + 1], scale=SCALE).then_inc(k_copied, 1)

                for k in range(KC):
                    act.wait_ge(start_loaded[k], 2 * DMA)
                    act.copy(wk_hi[:, k, :], wk_raw[:, k, :]).then_inc(start_hi_ready, 1)
                    act.copy(ctx_hi[0][:, k, 0:HR], ctx_raw[:, k, 0:HR]).then_inc(start_hi_ready, 1)
                high(0)
                act.wait_ge(bk_scaled, 1)
                for c in range(CHUNKS):
                    keys(c, 0)
                    if c == 0:
                        act.wait_ge(wv_loaded, DMA)
                        act.copy(wv_hi[:], wv_raw[:]).then_inc(wv_hi_ready, 1)
                    if c + 1 < CHUNKS:
                        high(c + 1)
                    keys(c, 1)
                    if c == 0:
                        act.wait_ge(wq_loaded, DMA)
                        act.copy(wq_hi[:], wk_raw[:]).then_inc(wq_hi_ready, 1)
                    if c == 1:
                        act.wait_ge(xT_loaded, DMA)
                        for k in range(KC):
                            act.copy(x_hi0[:, k, :], xT_raw[:, k, :]).then_inc(x_hi_ready, 1)

            @block.vector
            def _(dve):
                def low(c):
                    first = HR if c == 0 else 0
                    dve.wait_ge(ctx_hi_ready, c + 1)
                    dve.tensor_tensor(ctx_lo[c % 2][:, :, first:CR], ctx_raw[:, :, first:CR],
                                      ctx_hi[c % 2][:, :, first:CR], ALU.subtract).then_inc(ctx_lo_ready, 1)

                def values(c):
                    at_least(dve, v_stored, DMA * VT * c)
                    for j in range(VT):
                        n = v_n[j]
                        dve.wait_ge(v_done, c * VT + j + 1)
                        dve.tensor_tensor(v_out[0:n, j, :, 0:DH],
                                          v_ps[(c * VT + j) % 4][0:n, :].rearrange("p (h w) -> p h w", h=HEADS),
                                          bv_all[0:n, :].rearrange("p (h w) -> p h w", h=HEADS),
                                          ALU.add).then_inc(v_copied, 1)

                for k in range(KC):
                    dve.wait_ge(start_hi_ready, 2 * k + 1)
                    dve.tensor_tensor(wk_lo[:, k, :], wk_raw[:, k, :], wk_hi[:, k, :], ALU.subtract
                                      ).then_inc(start_lo_ready, 1)
                    dve.wait_ge(start_hi_ready, 2 * k + 2)
                    dve.tensor_tensor(ctx_lo[0][:, k, 0:HR], ctx_raw[:, k, 0:HR], ctx_hi[0][:, k, 0:HR],
                                      ALU.subtract).then_inc(start_lo_ready, 1)
                dve.wait_ge(bk_loaded, DMA)
                dve.tensor_scalar(bk_sc[:], bk_col[:], SCALE, None, ALU.mult).then_inc(bk_scaled, 1)
                low(0)
                dve.wait_ge(wv_hi_ready, 1)
                dve.tensor_tensor(wv_lo[:], wv_raw[:], wv_hi[:], ALU.subtract).then_inc(wv_lo_ready, 1)
                dve.wait_ge(bv_loaded, DMA)
                dve.wait_ge(ones_set, 1)
                for c in range(CHUNKS):
                    if c + 1 < CHUNKS:
                        low(c + 1)
                    values(c)

            @block.tensor
            def _(pe):
                terms = [(0, 1), (1, 0), (0, 0)]

                def key_products(c, half, m, k):
                    ctx_part = (ctx_hi[c % 2], ctx_lo[c % 2])
                    for n, (a, b) in enumerate(terms):
                        mm = pe.matmul(k_ps[m][:, 0:HR], (wk_hi, wk_lo)[a][:, k, P * m:P * m + P],
                                       ctx_part[b][:, k, half * HR:half * HR + HR],
                                       start=(k == 0 and n == 0), stop=(k == KC - 1 and n == 2))
                    if k == KC - 1:
                        mm.then_inc(k_done, 1)

                for k in range(KC):
                    pe.wait_ge(start_hi_ready, 2 * k + 2)
                    pe.wait_ge(start_lo_ready, 2 * k + 2)
                    for m in range(NG):
                        key_products(0, 0, m, k)
                for c in range(CHUNKS):
                    pe.wait_ge(ctx_hi_ready, c + 1)
                    pe.wait_ge(ctx_lo_ready, c + 1)
                    for half in range(1 if c == 0 else 0, 2):
                        for m in range(NG):
                            pe.wait_ge(k_copied, (2 * c + half - 1) * NG + m + 1)
                            for k in range(KC):
                                key_products(c, half, m, k)
                    if c == 0:
                        pe.wait_ge(wv_hi_ready, 1)
                        pe.wait_ge(wv_lo_ready, 1)
                    ctx_part = (ctx_hi[c % 2], ctx_lo[c % 2])
                    for j in range(VT):
                        at_least(pe, v_copied, c * VT + j - 3)
                        for k in range(KC):
                            for n, (a, b) in enumerate(terms):
                                mm = pe.matmul(v_ps[(c * VT + j) % 4][0:v_n[j], :],
                                               ctx_part[a][:, k, P * j:P * j + v_n[j]],
                                               (wv_hi, wv_lo)[b][:, k, :], start=(k == 0 and n == 0),
                                               stop=(k == KC - 1 and n == 2))
                        mm.then_inc(v_done, 1)

        k_loaded = sem("k_loaded")
        v_loaded = [sem(f"v_loaded_{i}") for i in range(3)]
        x_loaded = sem("x_loaded")
        out_stored = [sem(f"out_stored_{i}") for i in range(2)]
        q_done = sem("q_done")
        q_hi_ready = sem("q_hi_ready")
        q_lo_ready = sem("q_lo_ready")
        zeros_set = sem("zeros_set")
        bd_hi_ready = sem("bd_hi_ready")
        bd_lo_ready = sem("bd_lo_ready")
        scores_done = sem("scores_done")
        masked = sem("masked")
        max_ready = sem("max_ready")
        shifted = sem("shifted")
        exp_done = sem("exp_done")
        turned = sem("turned")
        pt_ready = sem("pt_ready")
        pv_done = sem("pv_done")
        inv_ready = sem("inv_ready")
        attn_ready = sem("attn_ready")
        resid_done = sem("resid_done")
        stats_done = sem("stats_done")
        meanvar_done = sem("meanvar_done")
        var_ready = sem("var_ready")
        half_set = sem("half_set")
        rstd_ready = sem("rstd_ready")
        shift_ready = sem("shift_ready")
        normed = sem("normed")
        scaled = sem("scaled")
        out_ready = sem("out_ready")
        row_scaled = sem("row_scaled")
        row_ready = sem("row_ready")
        last_shifted = sem("last_shifted")
        last_scaled = sem("last_scaled")
        last_ready = sem("last_ready")

        with ExitStack() as two:
            x_hi = [x_hi0, sb(two, "x_hi1", [P, KC, T], F32R)]
            x_lo = [x_lo0, sb(two, "x_lo1", [P, KC, T], F32R)]
            q_hi = sb(two, "q_hi", [P, NG, T], F32R)
            q_lo = sb(two, "q_lo", [P, NG, T], F32R)
            k_raw = sb(two, "k_raw", [P, NG, S], F32)
            bd_hi = [sb(two, f"bd_hi{i}", [P, NG, HG, S], F32R) for i in range(2)]
            bd_lo = [sb(two, f"bd_lo{i}", [P, NG, HG, S], F32R) for i in range(2)]
            probs = [sb(two, f"probs{h}", [P, TT, ROWS], F32) for h in range(2)]
            row_max = sb(two, "row_max", [P, 2 * TT, HH], F32)
            pt = [sb(two, f"pt{h}", [P, NT, T], F32) for h in range(2)]
            v_tiles = [sb(two, f"v_tiles{i}", [P, NT, VCOLS], F32) for i in range(3)]
            inv_sum = sb(two, "inv_sum", [P, 2 * TT, HH], F32)
            x_rows = sb(two, "x_rows", [P, TT, D], F32)
            attn = [sb(two, f"attn{i}", [P, TT, D], F32) for i in range(2)]
            y = [sb(two, f"y{i}", [P, TT, D], F32) for i in range(2)]
            stats = sb(two, "stats", [P, TT, 6], F32)
            meanvar = sb(two, "meanvar", [P, TT, 2], F32)
            var_eps = sb(two, "var_eps", [P, TT], F32)
            neg_mean = sb(two, "neg_mean", [P, TT], F32)
            minus_half = sb(two, "minus_half", [P, TT], F32)
            rstd = sb(two, "rstd", [P, TT], F32)
            shift = sb(two, "shift", [P, TT], F32)
            s_ps = [ps(two, f"s_ps{i}", [P, 2, BANK]) for i in range(2)]
            t_ps = [ps(two, f"t_ps{i}", [P, BANK]) for i in range(2)]
            q_ps = ps(two, "q_ps", [P, BANK])
            o_ps = ps(two, "o_ps", [P, BANK])

            def real(b):
                return not isinstance(b, int) or 0 <= b < B

            TURNS = ([], [0, 1], [2, 3], [4])

            def is_last(b):
                return isinstance(b, int) and b == B - 1

            def is_dve_row(b, t):
                return isinstance(b, int) and (b, t) == (B - 3, TT - 1)

            def v_buffer(b, h):
                return 2 if is_last(b) and h == 1 else h

            def pool_rows(b, t):
                return b * 4 + (t + 1) - (1 if isinstance(b, int) and b > B - 3 else 0)

            def bank_of(b, t):
                return q_ps if is_last(b) and t % 2 == 0 else o_ps

            def q_bank(b, g):
                return o_ps if isinstance(b, int) and b == 0 and g % 2 == 1 else q_ps

            def is_first_step(a):
                return isinstance(a, int) and a == -1

            def x_parts(a, s):
                if is_first_step(a):
                    return range(KC) if s == 7 else []
                return [s - 3] if 3 <= s <= 6 else []

            def steps(eng, body, first=-1):
                for a in range(first, 4):
                    body(a, a % 2)
                with eng.Fori(2, B // 2 - 1) as pair:
                    body(pair * 2, 0)
                    body(pair * 2 + 1, 1)
                for a in range(B - 2, B + 3):
                    body(a, a % 2)

            block = two.enter_context(nc.Block())

            @block.sync
            def _(sp):
                def load_v(b, h):
                    if v_buffer(b, h) < 2:
                        at_least(sp, pv_done, b * 8 + (4 * h - 4))
                    if isinstance(b, int) and b == 0:
                        sp.wait_ge(zeros_set, 7)
                    for i, row, hd, key, n in pieces:
                        col = (hd - first_head[i]) * VW
                        sp.dma_start(v_tiles[v_buffer(b, h)][row:row + n, i, col:col + VW],
                                     v_rows[b, key:key + n, HH * h + hd, :]).then_inc(v_loaded[v_buffer(b, h)], DMA)

                def store(b, t, par):
                    if is_last(b):
                        sp.wait_ge(last_ready, t + 1)
                    elif is_dve_row(b, t):
                        sp.wait_ge(row_ready, 1)
                    else:
                        sp.wait_ge(out_ready, pool_rows(b, t))
                    sp.dma_start(out[b, P * t:P * t + P, :], y[par][:, t, :]).then_inc(out_stored[par], DMA)

                def step(a, par):
                    if real(a + 2) and not (isinstance(a, int) and a == -2):
                        at_least(sp, x_hi_ready, a * 4 + 8)
                        at_least(sp, x_lo_ready, a * 4 + 8)
                        sp.dma_start(xT_raw[:], xT[a + 2].rearrange("(k p) t -> p k t", p=P)
                                     ).then_inc(xT_loaded, DMA)
                    if real(a - 1) and not is_last(a - 1):
                        load_v(a - 1, 1)
                    if real(a - 1):
                        at_least(sp, resid_done, a * 4 - 4)
                        sp.dma_start(x_rows[:], x[a - 1].rearrange("(t p) d -> p t d", p=P)
                                     ).then_inc(x_loaded, DMA)
                    if real(a - 3):
                        store(a - 3, 2, 1 - par)
                        store(a - 3, 3, 1 - par)
                    if real(a):
                        load_v(a, 0)
                    if is_last(a):
                        load_v(a, 1)
                    if real(a - 2):
                        store(a - 2, 0, par)
                    if real(a + 2):
                        at_least(sp, bd_hi_ready, a * 4 + 8)
                        at_least(sp, bd_lo_ready, a * 4 + 8)
                        sp.dma_start(k_raw[:], k_dram[a + 2]).then_inc(k_loaded, DMA)
                    if real(a - 2):
                        store(a - 2, 1, par)
                steps(sp, step, first=-2)
                for par in range(2):
                    sp.wait_ge(out_stored[par], DMA * TT * B // 2)

            @block.tensor
            def _(pe):
                terms = [(0, 1), (1, 0), (0, 0)]

                def q_half(b, g, part, par):
                    if part == 0:
                        pe.wait_ge(x_hi_ready, b * 4 + 4)
                        pe.wait_ge(x_lo_ready, b * 4 + 4)
                        used = b * 4 + g
                        if isinstance(used, int) and used <= 4:
                            used -= 1
                        at_least(pe, q_hi_ready, used)
                        at_least(pe, q_lo_ready, used)
                    x_part = (x_hi[par], x_lo[par])
                    for k in (2 * part, 2 * part + 1):
                        for n, (u, v) in enumerate(terms):
                            mm = pe.matmul(q_bank(b, g)[:, :], (wq_hi, wq_lo)[u][:, k, P * g:P * g + P],
                                           x_part[v][:, k, :], start=(k == 0 and n == 0),
                                           stop=(k == KC - 1 and n == 2))
                    if part == 1:
                        mm.then_inc(q_done, 1)

                def scores(b, h, t, par):
                    pe.wait_ge(q_hi_ready, b * 4 + (2 * h + 2))
                    pe.wait_ge(q_lo_ready, b * 4 + (2 * h + 2))
                    pe.wait_ge(bd_hi_ready, b * 4 + 4)
                    pe.wait_ge(bd_lo_ready, b * 4 + 4)
                    at_least(pe, masked, b * 8 + (4 * h + t - 1))
                    for j in range(2):
                        g = 2 * h + j
                        for n, (u, v) in enumerate(terms):
                            mm = pe.matmul(s_ps[t % 2][:, j, 0:GS], (q_hi, q_lo)[u][:, g, P * t:P * t + P],
                                           (bd_hi, bd_lo)[v][par][:, g, :, :].rearrange("p h s -> p (h s)"),
                                           start=(n == 0), stop=(n == 2))
                    mm.then_inc(scores_done, 1)

                def turn(b, h, i):
                    pe.wait_ge(exp_done, b * 8 + (4 * h + 4))
                    at_least(pe, pt_ready, b * (2 * NT) + (NT * h + i - 1))
                    w = tile_rows[i]
                    for t in range(TT):
                        mm = pe.transpose(t_ps[(NT * h + i) % 2][0:w, P * t:P * t + P],
                                          probs[h][:, t, P * i:P * i + w], ident[:, :])
                    mm.then_inc(turned, 1)

                def product(b, h, t):
                    pe.wait_ge(pt_ready, b * (2 * NT) + (NT * h + NT))
                    if v_buffer(b, h) == 2:
                        pe.wait_ge(v_loaded[2], DMA * len(pieces))
                    else:
                        pe.wait_ge(v_loaded[h], (b + 1) * (DMA * len(pieces)))
                    at_least(pe, attn_ready, b * 8 + (4 * h + t) - (1 if is_last(b) else 0))
                    for i in range(NT):
                        w, col = tile_rows[i], first_head[i] * VW
                        mm = pe.matmul(bank_of(b, t)[:, col:col + tile_cols[i]], pt[h][0:w, i, P * t:P * t + P],
                                       v_tiles[v_buffer(b, h)][0:w, i, 0:tile_cols[i]], start=(i == 0),
                                       stop=(i == NT - 1), skip_group_check=True)
                    mm.then_inc(pv_done, 1)

                def step(a, par):
                    for s in range(8):
                        h, t = s // 4, s % 4
                        qb = a + h
                        if real(qb):
                            q_half(qb, (2 if h == 0 else 0) + t // 2, t % 2, (par + h) % 2)
                        if real(a):
                            scores(a, h, t, par)
                        last_turns = is_last(a - 1) and h == 0
                        if last_turns:
                            product(a - 1, h, t)
                        if real(a - 1 + h):
                            for i in TURNS[t]:
                                turn(a - 1 + h, 1 - h, i)
                        if real(a - 1) and not last_turns:
                            product(a - 1, h, t)

                steps(pe, step)

            @block.vector
            def _(dve):
                def o_heads(b, t):
                    return bank_of(b, t)[:, 0:HH * VW].rearrange("p (h w) -> p h w", w=VW)

                dve.memset(bd_hi[0][:].bitcast(F32), 0.0).then_inc(zeros_set, 1)
                dve.memset(bd_hi[1][:].bitcast(F32), 0.0).then_inc(zeros_set, 1)

                def subtract_last_max():
                    u = 2 * TT - 1
                    dve.wait_ge(max_ready, B * 8)
                    v = probs[1][:, TT - 1, :].rearrange("p (h s) -> p h s", h=HH)
                    dve.tensor_tensor(v, v, row_max[:, u, :].unsqueeze(2).broadcast_to([P, HH, S]),
                                      ALU.subtract).then_inc(last_shifted, 1)

                def invert_sums(b, h, t):
                    u = 4 * h + t
                    dve.wait_ge(pv_done, b * 8 + (u + 1))
                    dve.reciprocal(inv_sum[:, u, :], o_heads(b, t)[:, :, DH]).then_inc(inv_ready, 1)

                def scale_attn(b, h, t, par):
                    u = 4 * h + t
                    dve.wait_ge(inv_ready, b * 8 + (u + 1))
                    if h == 0:
                        if isinstance(b, int) and is_dve_row(b - 2, t):
                            dve.wait_ge(row_scaled, 1)
                        else:
                            at_least(dve, scaled, b * 4 + (t - 7))
                    dve.tensor_tensor(attn[par][:, t, HH * DH * h:HH * DH * (h + 1)].rearrange(
                                          "p (h w) -> p h w", w=DH),
                                      o_heads(b, t)[:, :, 0:DH],
                                      inv_sum[:, u, :].unsqueeze(2).broadcast_to([P, HH, DH]),
                                      ALU.mult).then_inc(attn_ready, 1)

                def row_stats(b, t, par):
                    dve.wait_ge(resid_done, b * 4 + (t + 1))
                    dve.bn_stats(stats[:, t, :], attn[par][:, t, :]).then_inc(stats_done, 1)

                def mean_and_var(b, t):
                    dve.bn_aggr(meanvar[:, t, :], stats[:, t, :]).then_inc(meanvar_done, 1)

                def row_factors(b):
                    dve.wait_ge(meanvar_done, b * 4 + 4)
                    at_least(dve, normed, b * 4)
                    dve.tensor_scalar(var_eps[:], meanvar[:, :, 1], LN_EPS, None, ALU.add
                                      ).then_inc(var_ready, 1)
                    dve.tensor_scalar(neg_mean[:], meanvar[:, :, 0], -1.0, None, ALU.mult
                                      ).then_inc(var_ready, 1)

                def scale_row(b, t, par):
                    dve.wait_ge(normed, b * 4 + (t + 1))
                    dve.wait_ge(out_stored[par], DMA * TT * (b // 2))
                    dve.tensor_tensor(y[par][:, t, :], attn[par][:, t, :], gamma_all[:], ALU.mult
                                      ).then_inc(row_scaled, 1)
                    dve.wait_ge(row_scaled, 1)
                    dve.tensor_tensor(y[par][:, t, :], y[par][:, t, :], beta_all[:], ALU.add
                                      ).then_inc(row_ready, 1)

                def add_row(b, t, par):
                    dve.wait_ge(attn_ready, b * 8 + (5 + t))
                    dve.wait_ge(x_loaded, b * DMA + DMA)
                    dve.tensor_tensor(attn[par][:, t, :], attn[par][:, t, :], x_rows[:, t, :], ALU.add
                                      ).then_inc(resid_done, 1)

                def finish_output(par):
                    dve.wait_ge(var_ready, B * 2)
                    dve.wait_ge(out_stored[par], DMA * TT * ((B - 1) // 2))
                    for t in range(TT):
                        dve.scalar_tensor_tensor(out=y[par][:, t, :], in0=attn[par][:, t, :],
                                                 scalar=neg_mean[:, t:t + 1], in1=gamma_all[:],
                                                 op0=ALU.add, op1=ALU.mult).then_inc(last_scaled, 1)
                    dve.wait_ge(rstd_ready, B)
                    for t in range(TT):
                        dve.wait_ge(last_scaled, t + 1)
                        dve.scalar_tensor_tensor(out=y[par][:, t, :], in0=y[par][:, t, :],
                                                 scalar=rstd[:, t:t + 1], in1=beta_all[:],
                                                 op0=ALU.mult, op1=ALU.add).then_inc(last_ready, 1)

                def split_x(b, k, par):
                    dve.wait_ge(x_hi_ready, b * 4 + (k + 1))
                    dve.tensor_tensor(x_lo[par][:, k, :], xT_raw[:, k, :], x_hi[par][:, k, :], ALU.subtract
                                      ).then_inc(x_lo_ready, 1)

                def low_keys(b, q, par):
                    rows = slice(DH * q, DH * q + DH)
                    dve.wait_ge(bd_hi_ready, b * 4 + (q + 1))
                    dve.tensor_tensor(bd_lo[par][rows, :, q, :], k_raw[rows, :, :], bd_hi[par][rows, :, q, :],
                                      ALU.subtract).then_inc(bd_lo_ready, 1)

                def q_low(b, g):
                    dve.wait_ge(q_hi_ready, b * 4 + (g + 1))
                    dve.scalar_tensor_tensor(out=q_lo[:, g, :], in0=q_bank(b, g)[:, :], scalar=bq_col[:, g:g + 1],
                                             in1=q_hi[:, g, :], op0=ALU.add, op1=ALU.subtract
                                             ).then_inc(q_lo_ready, 1)

                def add_mask(b, h, t, par):
                    u = 4 * h + t
                    dve.wait_ge(scores_done, b * 8 + (u + 1))
                    if t == 0:
                        at_least(dve, turned, b * (2 * NT) + (NT * h - NT))
                    dve.tensor_tensor(probs[h][:, t, :].rearrange("p (j c) -> p j c", j=2),
                                      s_ps[t % 2][:, :, 0:GS],
                                      mask_pad[par][:, ROWS * h:ROWS * h + ROWS].rearrange("p (j c) -> p j c", j=2),
                                      ALU.add).then_inc(masked, 1)

                def maximum(b, h, t):
                    u = 4 * h + t
                    dve.wait_ge(masked, b * 8 + (u + 1))
                    dve.tensor_reduce(row_max[:, u, :], probs[h][:, t, :].rearrange("p (h s) -> p h s", h=HH),
                                      AX.X, ALU.max).then_inc(max_ready, 1)

                def step(a, par):
                    for s in range(8):
                        h, t = s // 4, s % 4
                        last = None
                        if s == 0 and real(a - 2):
                            last = (a - 2, 1, 3)
                        if s > 0 and real(a - 1):
                            last = (a - 1, (s - 1) // 4, (s - 1) % 4)
                        if last is not None:
                            invert_sums(*last)
                        if 1 <= s <= 4 and real(a + 1):
                            low_keys(a + 1, s - 1, 1 - par)
                        if (is_last(a - 1) and s >= 6) or (is_last(a - 2) and s == 0):
                            add_row(B - 1, (s - 6) % 8, (B - 1) % 2)
                        if last is not None:
                            scale_attn(*last, par if s == 0 else 1 - par)
                        if (is_last(a - 1) and s >= 6) or (is_last(a - 2) and s == 0):
                            t_end = (s - 6) % 8
                            row_stats(B - 1, t_end, (B - 1) % 2)
                            if s == 0:
                                add_row(B - 1, TT - 1, (B - 1) % 2)
                            dve.wait_ge(stats_done, (B - 1) * 4 + (t_end + 1))
                            mean_and_var(B - 1, t_end)
                            if s == 0:
                                row_stats(B - 1, TT - 1, (B - 1) % 2)
                                dve.wait_ge(stats_done, B * 4)
                                mean_and_var(B - 1, TT - 1)
                                row_factors(B - 1)
                                finish_output((B - 1) % 2)
                        if is_last(a - 1) and s == 0:
                            scale_row(B - 3, TT - 1, 1 - par)
                        rows = None
                        if real(a - 2) and s < 2 and not is_last(a - 2):
                            rows = (a - 2, 2 + s)
                            row_stats(*rows, par)
                        if real(a - 1) and s >= 6 and not is_last(a - 1):
                            rows = (a - 1, s - 6)
                            row_stats(*rows, 1 - par)
                        if s == 3 and real(a + 2):
                            for k in x_parts(a, s):
                                split_x(a + 2, k, par)
                        if real(a + h) and t % 2 == 1:
                            q_low(a + h, (2 if h == 0 else 0) + t // 2)
                        if real(a):
                            add_mask(a, h, t, par)
                        if s >= 4 and real(a + 2):
                            for k in x_parts(a, s):
                                split_x(a + 2, k, par)
                        if rows is not None:
                            dve.wait_ge(stats_done, rows[0] * 4 + (rows[1] + 1))
                        if real(a):
                            maximum(a, h, t)
                        if is_last(a) and s == 7:
                            subtract_last_max()
                        if rows is not None:
                            mean_and_var(*rows)
                        if s == 1 and real(a - 2) and not is_last(a - 2):
                            row_factors(a - 2)

                steps(dve, step)

            @block.gpsimd
            def _(pool):
                def add_rows(b, t, par):
                    pool.wait_ge(attn_ready, b * 8 + (5 + t))
                    pool.wait_ge(x_loaded, b * DMA + DMA)
                    pool.tensor_tensor(attn[par][:, t, :], attn[par][:, t, :], x_rows[:, t, :], ALU.add
                                       ).then_inc(resid_done, 1)

                def scale_rows(b, t, par):
                    pool.wait_ge(normed, b * 4 + (t + 1))
                    if t == 0:
                        at_least(pool, out_stored[par], b * (DMA * TT // 2) - par * (DMA * TT // 2))
                    pool.tensor_tensor(y[par][:, t, :], attn[par][:, t, :], gamma_all[:], ALU.mult
                                       ).then_inc(scaled, 1)
                    pool.wait_ge(scaled, pool_rows(b, t))
                    pool.tensor_tensor(y[par][:, t, :], y[par][:, t, :], beta_all[:], ALU.add).then_inc(out_ready, 1)

                def row_factors(b):
                    pool.wait_ge(var_ready, b * 2 + 2)
                    pool.tensor_tensor(rstd[:], var_eps[:], minus_half[:], ALU.pow).then_inc(rstd_ready, 1)
                    pool.wait_ge(rstd_ready, b + 1)
                    pool.tensor_tensor(shift[:], neg_mean[:], rstd[:], ALU.mult).then_inc(shift_ready, 1)

                pool.memset(bd_lo[0][:].bitcast(F32), 0.0).then_inc(zeros_set, 1)
                pool.memset(bd_lo[1][:].bitcast(F32), 0.0).then_inc(zeros_set, 1)
                pool.memset(v_tiles[0][:], 0.0).then_inc(zeros_set, 1)
                pool.memset(v_tiles[1][:], 0.0).then_inc(zeros_set, 1)
                pool.memset(v_tiles[2][:], 0.0).then_inc(zeros_set, 1)
                pool.memset(minus_half[:], -0.5).then_inc(half_set, 1)
                pool.wait_ge(half_set, 1)

                def subtract_max(b, h, t):
                    u = 4 * h + t
                    pool.wait_ge(max_ready, b * 8 + (u + 1))
                    v = probs[h][:, t, :].rearrange("p (h s) -> p h s", h=HH)
                    pool.tensor_tensor(v, v, row_max[:, u, :].unsqueeze(2).broadcast_to([P, HH, S]),
                                       ALU.subtract).then_inc(shifted, 1)

                def step(a, par):
                    for s in range(8):
                        if s == 0:
                            if real(a - 1) and not is_last(a - 1):
                                subtract_max(a - 1, 1, 3)
                        elif real(a):
                            subtract_max(a, (s - 1) // 4, (s - 1) % 4)
                        if s == 0 and real(a - 2) and not is_last(a - 2):
                            add_rows(a - 2, 3, par)
                        if s >= 5 and real(a - 1) and not is_last(a - 1):
                            add_rows(a - 1, s - 5, 1 - par)
                        if s == (4 if is_last(a - 2) else 2) and real(a - 2):
                            row_factors(a - 2)
                        if s in (1, 3) and real(a - 3) and not is_last(a - 3) and not is_dve_row(a - 3, (s + 3) // 2):
                            scale_rows(a - 3, (s + 3) // 2, 1 - par)
                        if s in (4, 7) and real(a - 2) and not is_last(a - 2):
                            scale_rows(a - 2, s // 7, par)

                steps(pool, step)

            @block.scalar
            def _(act):
                def exponent(b, h, t):
                    if is_last(b) and (h, t) == (1, TT - 1):
                        act.wait_ge(last_shifted, 1)
                    else:
                        act.wait_ge(shifted, b * 8 + (4 * h + t + 1))
                    act.activation(probs[h][:, t, :], probs[h][:, t, :], ACT.Exp).then_inc(exp_done, 1)

                def high_x(b, k, par):
                    if k == 0:
                        act.wait_ge(xT_loaded, b * DMA + DMA)
                        at_least(act, scores_done, b * 8 - 13)
                    if k == 2:
                        at_least(act, q_done, b * 4 - 4)
                    act.copy(x_hi[par][:, k, :], xT_raw[:, k, :]).then_inc(x_hi_ready, 1)

                def high_keys(b, q, par):
                    rows = slice(DH * q, DH * q + DH)
                    if q == 0:
                        act.wait_ge(k_loaded, b * DMA + DMA)
                        at_least(act, scores_done, b * 8 - 8)
                        if isinstance(b, int) and b < 2:
                            act.wait_ge(zeros_set, 7)
                    act.copy(bd_hi[par][rows, :, q, :], k_raw[rows, :, :]).then_inc(bd_hi_ready, 1)

                def high_q(b, g):
                    act.wait_ge(q_done, b * 4 + (g + 1))
                    act.activation(q_hi[:, g, :], q_bank(b, g)[:, :], ACT.Identity, bias=bq_col[:, g:g + 1]
                                   ).then_inc(q_hi_ready, 1)

                def copy_pt(b, h, i):
                    act.wait_ge(turned, b * (2 * NT) + (NT * h + i + 1))
                    w = tile_rows[i]
                    act.copy(pt[h][0:w, i, :], t_ps[(NT * h + i) % 2][0:w, :]).then_inc(pt_ready, 1)

                def norm(b, t, par):
                    act.wait_ge(shift_ready, b + 1)
                    act.activation(attn[par][:, t, :], attn[par][:, t, :], ACT.Identity,
                                   bias=shift[:, t:t + 1], scale=rstd[:, t:t + 1]).then_inc(normed, 1)

                def step(a, par):
                    for s in range(8):
                        h, t = s // 4, s % 4
                        if real(a + 2) and not is_first_step(a):
                            for k in x_parts(a, s):
                                high_x(a + 2, k, par)
                        if h == 0 and real(a + 1):
                            high_keys(a + 1, t, 1 - par)
                        if t % 2 == 1 and real(a + h):
                            high_q(a + h, (2 if h == 0 else 0) + t // 2)
                        if real(a + 2) and is_first_step(a):
                            for k in x_parts(a, s):
                                high_x(a + 2, k, par)
                        if s == 0:
                            if real(a - 1):
                                exponent(a - 1, 1, 3)
                        elif real(a):
                            exponent(a, (s - 1) // 4, (s - 1) % 4)
                        if real(a - 1 + h):
                            for i in TURNS[t]:
                                copy_pt(a - 1 + h, 1 - h, i)
                        if 3 <= s <= 6 and real(a - 2) and not is_last(a - 2):
                            norm(a - 2, s - 3, par)

                steps(act, step)


def kernel(x, ctx_1024, mask_BxS2_ik0, L0_xattn_edge_fea, L0_xattn_wq, L0_xattn_bq, L0_xattn_wk,
           L0_xattn_bk, L0_xattn_wv, L0_xattn_bv, L0_xattn_gamma, L0_xattn_beta):
    import numpy as np
    import concourse.bacc as bacc
    from concourse.bass_utils import run_bass_kernel_spmd

    c = np.ascontiguousarray
    B, T, D = x.shape
    S = ctx_1024.shape[1]
    assert B == 2 * HEADS

    def in_turns(a):
        a = np.asarray(a)
        return a.reshape(2, B // 2, *a.shape[1:]).swapaxes(0, 1).reshape(a.shape)

    x = in_turns(x)
    ctx = in_turns(ctx_1024)
    arrays = {
        "x": c(x),
        "xT": c(x.transpose(0, 2, 1)),
        "ctxT": c(ctx.reshape(B * S, D).T.reshape(D, B // 8, 8 * S)),
        "mask": c(np.asarray(mask_BxS2_ik0).reshape(HEADS, 2, S).swapaxes(0, 1).reshape(2, HEADS * S)),
        "wqT": c(np.asarray(L0_xattn_wq).T),
        "bq": c(np.asarray(L0_xattn_bq).reshape(D // 128, 128).T),
        "wkT": c(np.asarray(L0_xattn_wk).T),
        "bk": c(np.asarray(L0_xattn_bk).reshape(D // 128, 128).T),
        "wvT": c(np.asarray(L0_xattn_wv).T),
        "bv": c(np.asarray(L0_xattn_bv)),
        "gamma": c(np.asarray(L0_xattn_gamma)),
        "beta": c(np.asarray(L0_xattn_beta)),
    }
    nc = bacc.Bacc("TRN2", target_bir_lowering=False, num_devices=1)
    args = [nc.dram_tensor(f"in_{n}", a.shape, mybir.dt.from_np(a.dtype), kind="ExternalInput").ap()
            for n, a in arrays.items()]
    args.append(nc.dram_tensor("out_0", (B, T, D), F32, kind="ExternalOutput").ap())
    xattn(nc, *args)
    r = run_bass_kernel_spmd(nc, [{f"in_{n}": a for n, a in arrays.items()}], core_ids=[0])
    out = r.results[0]["out_0"]
    return c(out.reshape(B // 2, 2, T, D).swapaxes(0, 1).reshape(B, T, D))
```
